# Optimizing a Trainium2 kernel written in Bass

```python
import numpy as np
import jax
import jax.numpy as jnp

def _softmax(x, axis=-1):
    return jax.nn.softmax(x, axis=axis)

def _gelu(x):
    return jax.nn.gelu(x, approximate=True)

def _silu(x):
    return jax.nn.silu(x)

def _sigmoid(x):
    return jax.nn.sigmoid(x)

def _layernorm(x, axis=-1, eps=1e-05):
    m = jnp.mean(x, axis=axis, keepdims=True)
    v = jnp.var(x, axis=axis, keepdims=True)
    return (x - m) / jnp.sqrt(v + eps)

def _scatter_add(tgt, idx, src, axis=0):
    return tgt.at[idx].add(src)

def _segment_sum(src, seg, n):
    return jax.ops.segment_sum(src, seg, n)
kernel_name = 'mk_macaron_d1_jaxref_r2_cab18e'

def setup_inputs(seed: int=0):
    np.random.seed(seed)
    _w = jnp.asarray

    def _L0_attn_setup():
        import jax, jax.numpy as jnp
        import numpy as np
        D_MODEL, D_STATE, D_CONV, D_INNER = (512, 16, 4, 1024)
        BATCH, SEQ = (2, 1024)

        def _silu(x):
            return x * jax.nn.sigmoid(x)

        def _selective_scan(u, delta, Bm, Cm, A):

            def step(h, t):
                delta_t, B_t, C_t, u_t = t
                dA = jnp.exp(delta_t[:, :, None] * A[None, :, :])
                dBu = delta_t[:, :, None] * B_t[:, None, :] * u_t[:, :, None]
                h = dA * h + dBu
                y = jnp.einsum('bds,bs->bd', h, C_t)
                return (h, y)
            b = u.shape[0]
            h0 = jnp.zeros((b, u.shape[2], A.shape[1]), dtype=u.dtype)
            xs = (jnp.swapaxes(delta, 0, 1), jnp.swapaxes(Bm, 0, 1), jnp.swapaxes(Cm, 0, 1), jnp.swapaxes(u, 0, 1))
            _, ys = jax.lax.scan(step, h0, xs)
            return jnp.swapaxes(ys, 0, 1)
        key = jax.random.key(seed)
        ks = jax.random.split(key, 8)
        inp = jax.random.normal(ks[0], (BATCH, SEQ, D_MODEL), dtype=jnp.float32)
        W_in = jax.random.normal(ks[1], (D_MODEL, 2 * D_INNER), dtype=jnp.float32) * 0.02
        conv_w = jax.random.normal(ks[2], (D_CONV, 1, D_INNER), dtype=jnp.float32) * 0.1
        conv_b = jnp.zeros((D_INNER,), dtype=jnp.float32)
        W_x = jax.random.normal(ks[3], (D_INNER, 2 * D_STATE), dtype=jnp.float32) * 0.02
        W_dt = jax.random.normal(ks[4], (D_INNER, D_INNER), dtype=jnp.float32) * 0.02
        b_dt = jnp.zeros((D_INNER,), dtype=jnp.float32)
        W_out = jax.random.normal(ks[5], (D_INNER, D_MODEL), dtype=jnp.float32) * 0.02
        A = -0.5 * jnp.tile(jnp.arange(1, D_STATE + 1, dtype=jnp.float32)[None, :], (D_INNER, 1))
        D = jnp.ones((D_INNER,), dtype=jnp.float32)
        return {'inp': inp, 'W_in': W_in, 'conv_w': conv_w, 'conv_b': conv_b, 'W_x': W_x, 'W_dt': W_dt, 'b_dt': b_dt, 'W_out': W_out, 'A': A, 'D': D}
    _L0_attn_in = _L0_attn_setup()

    def _L0_ffn_setup():
        import jax, jax.numpy as jnp
        import numpy as np
        DIM = 512

        def _reference_tuple_inner(x, W_r, W_k, W_v, mu_r, mu_k):
            B, T, C = x.shape
            x_prev = jnp.concatenate([jnp.zeros((B, 1, C), x.dtype), x[:, :-1, :]], axis=1)
            xr = mu_r * x + (1.0 - mu_r) * x_prev
            xk = mu_k * x + (1.0 - mu_k) * x_prev
            r = jax.nn.sigmoid(jnp.einsum('btc,dc->btd', xr, W_r))
            k = jnp.einsum('btc,dc->btd', xk, W_k)
            k_act = jnp.square(jax.nn.relu(k))
            out = r * jnp.einsum('btc,dc->btd', k_act, W_v)
            new_state = x[:, -1, :]
            return (out, new_state)
        key = jax.random.key(seed)
        ks = jax.random.split(key, 6)
        B, T, C = (8, 1024, DIM)
        x = jax.random.normal(ks[0], (B, T, C), dtype=jnp.float32)
        s = 1.0 / np.sqrt(C)
        W_r = jax.random.uniform(ks[1], (C, C), jnp.float32, -s, s)
        W_k = jax.random.uniform(ks[2], (C, C), jnp.float32, -s, s)
        W_v = jax.random.uniform(ks[3], (C, C), jnp.float32, -s, s)
        mu_r = jax.random.uniform(ks[4], (C,), jnp.float32)
        mu_k = jax.random.uniform(ks[5], (C,), jnp.float32)
        return {'x': x, 'W_r': W_r, 'W_k': W_k, 'W_v': W_v, 'mu_r': mu_r, 'mu_k': mu_k}
    _L0_ffn_in = _L0_ffn_setup()
    _d = {'L0_attn_inp': _L0_attn_in['inp'], 'L0_attn_W_in': _L0_attn_in['W_in'], 'L0_attn_conv_w': _L0_attn_in['conv_w'], 'L0_attn_conv_b': _L0_attn_in['conv_b'], 'L0_attn_W_x': _L0_attn_in['W_x'], 'L0_attn_W_dt': _L0_attn_in['W_dt'], 'L0_attn_b_dt': _L0_attn_in['b_dt'], 'L0_attn_W_out': _L0_attn_in['W_out'], 'L0_attn_A': _L0_attn_in['A'], 'L0_attn_D': _L0_attn_in['D'], 'L0_ffn_W_r': _L0_ffn_in['W_r'], 'L0_ffn_W_k': _L0_ffn_in['W_k'], 'L0_ffn_W_v': _L0_ffn_in['W_v'], 'L0_ffn_mu_r': _L0_ffn_in['mu_r'], 'L0_ffn_mu_k': _L0_ffn_in['mu_k']}
    _x0 = _d['L0_attn_inp']
    _d['L0_attn_inp'] = jax.random.normal(jax.random.fold_in(jax.random.key(seed), 1), (4, 2048, 512), dtype=_x0.dtype)
    del _x0
    return _d

def reference(L0_attn_inp, L0_attn_W_in, L0_attn_conv_w, L0_attn_conv_b, L0_attn_W_x, L0_attn_W_dt, L0_attn_b_dt, L0_attn_W_out, L0_attn_A, L0_attn_D, L0_ffn_W_r, L0_ffn_W_k, L0_ffn_W_v, L0_ffn_mu_r, L0_ffn_mu_k):

    def _L0_attn_ref(inp, W_in, conv_w, conv_b, W_x, W_dt, b_dt, W_out, A, D):
        import jax, jax.numpy as jnp
        import numpy as np
        D_MODEL, D_STATE, D_CONV, D_INNER = (512, 16, 4, 1024)
        BATCH, SEQ = (2, 1024)

        def _silu(x):
            return x * jax.nn.sigmoid(x)

        def _selective_scan(u, delta, Bm, Cm, A):

            def step(h, t):
                delta_t, B_t, C_t, u_t = t
                dA = jnp.exp(delta_t[:, :, None] * A[None, :, :])
                dBu = delta_t[:, :, None] * B_t[:, None, :] * u_t[:, :, None]
                h = dA * h + dBu
                y = jnp.einsum('bds,bs->bd', h, C_t)
                return (h, y)
            b = u.shape[0]
            h0 = jnp.zeros((b, u.shape[2], A.shape[1]), dtype=u.dtype)
            xs = (jnp.swapaxes(delta, 0, 1), jnp.swapaxes(Bm, 0, 1), jnp.swapaxes(Cm, 0, 1), jnp.swapaxes(u, 0, 1))
            _, ys = jax.lax.scan(step, h0, xs)
            return jnp.swapaxes(ys, 0, 1)
        residual = inp
        x_in = inp - jnp.mean(inp, axis=-1, keepdims=True)
        xz = x_in @ W_in
        x, z = jnp.split(xz, 2, axis=-1)
        x = jax.lax.conv_general_dilated(x, conv_w, window_strides=(1,), padding=[(1, 2)], dimension_numbers=('NWC', 'WIO', 'NWC'), feature_group_count=D_INNER) + conv_b
        x = _silu(x)
        x_db = x @ W_x
        Bm, Cm = jnp.split(x_db, 2, axis=-1)
        delta = jax.nn.softplus(x @ W_dt + b_dt)
        y = _selective_scan(x, delta, Bm, Cm, A)
        y = y + x * D[None, None, :]
        y = y * _silu(z)
        out = y @ W_out
        return out + residual

    def _L0_ffn_ref(x, W_r, W_k, W_v, mu_r, mu_k):
        import jax, jax.numpy as jnp
        import numpy as np
        DIM = 512

        def _reference_tuple_inner(x, W_r, W_k, W_v, mu_r, mu_k):
            B, T, C = x.shape
            x_prev = jnp.concatenate([jnp.zeros((B, 1, C), x.dtype), x[:, :-1, :]], axis=1)
            xr = mu_r * x + (1.0 - mu_r) * x_prev
            xk = mu_k * x + (1.0 - mu_k) * x_prev
            r = jax.nn.sigmoid(jnp.einsum('btc,dc->btd', xr, W_r))
            k = jnp.einsum('btc,dc->btd', xk, W_k)
            k_act = jnp.square(jax.nn.relu(k))
            out = r * jnp.einsum('btc,dc->btd', k_act, W_v)
            new_state = x[:, -1, :]
            return (out, new_state)
        return _reference_tuple_inner(x, W_r, W_k, W_v, mu_r, mu_k)[0]
    x = L0_attn_inp
    x = x + 0.5 * _L0_ffn_ref(_layernorm(x, axis=-1), L0_ffn_W_r, L0_ffn_W_k, L0_ffn_W_v, L0_ffn_mu_r, L0_ffn_mu_k)
    x = x + _L0_attn_ref(_layernorm(x, axis=-1), L0_attn_W_in, L0_attn_conv_w, L0_attn_conv_b, L0_attn_W_x, L0_attn_W_dt, L0_attn_b_dt, L0_attn_W_out, L0_attn_A, L0_attn_D)
    x = x + 0.5 * _L0_ffn_ref(_layernorm(x, axis=-1), L0_ffn_W_r, L0_ffn_W_k, L0_ffn_W_v, L0_ffn_mu_r, L0_ffn_mu_k)
    return x

_drawn_inputs = setup_inputs


def setup_inputs(seed=0):
    import zlib

    import numpy as np

    out = dict(_drawn_inputs(seed))
    spreads = {'L0_attn_conv_b': (0.0, 0.1), 'L0_attn_b_dt': (0.0, 0.1), 'L0_attn_D': (1.0, 0.2)}
    factors = {}
    for name, (base, spread) in spreads.items():
        noise = np.random.default_rng([zlib.crc32(name.encode()), seed]).standard_normal(out[name].shape)
        drawn = base * np.exp(spread * noise) if base else spread * noise
        out[name] = jnp.asarray(drawn.astype(out[name].dtype))
    for name, factor in factors.items():
        out[name] = (out[name] * factor).astype(out[name].dtype)
    return out
```

```python
from contextlib import ExitStack

import concourse.bass as bass
from concourse import mybir

F32 = mybir.dt.float32
ALU = mybir.AluOpType
ACT = mybir.ActivationFunctionType

P = 128
BATCH, SEQ, DM = 4, 2048, 512
DI, DS, KC = 1024, 16, 4
EPS = 1e-5
NB = DM // P
ND = DI // P
PAD_L, PAD_R = 1, 2

FT = 512
FJ = FT // P
FC = SEQ // FT
NX = FC

T = 256
TJ = T // P
TH = T + PAD_L + PAD_R
MC = SEQ // T
SG = 4
NG = DS // SG
NU = NG * ND
NH = 4
ROW = SEQ + PAD_L + PAD_R
TAIL = T + TH


def ffn_phase(nc, name, x_in, w_r, w_k, w_v, mu_r, mu_k, out, hT_pad=None):
    mixer = hT_pad is not None
    x_v = x_in.rearrange("b (c j p) d -> (b c) p j d", c=FC, p=P)
    out_v = out.rearrange("b (c j p) d -> (b c) p j d", c=FC, p=P)

    with ExitStack() as ctx:
        def sb(n, shape):
            return ctx.enter_context(nc.sbuf_tensor(f"{name}_{n}", shape, F32))

        def sem(n):
            return ctx.enter_context(nc.semaphore(f"{name}_{n}"))

        ident = sb("ident", [P, P])
        w_nat = sb("w_nat", [P, 3, NB, DM])
        wT = sb("wT", [P, 3, NB, DM])
        mu = sb("mu", [P, 2, NB])
        half = sb("half", [P, FJ])
        x = sb("x", [P, NX, FJ, DM])
        stats = sb("stats", [P, FJ, 6])
        mv = sb("mv", [P, 2, FJ, 2])
        ve = sb("ve", [P, 2, FJ])
        rstd = sb("rstd", [P, 2, FJ])
        mark = sb("mark", [P, 1])
        hx = sb("hx", [P, FJ, DM])
        xhT = sb("xhT", [P, 2, NB, FT + 1])
        dsh = sb("dsh", [P, NB, FT])
        xr = sb("xr", [P, NB, FT])
        xk = sb("xk", [P, NB, FT])
        ka = sb("ka", [P, NB, FT])
        rt = sb("rt", [P, FJ, DM])
        h2 = sb("h2", [P, FJ, DM]) if mixer else None
        h2T = sb("h2T", [P, NB, FT]) if mixer else None
        zpad = sb("zpad", [P, NB, TAIL]) if mixer else None

        ps_kr = [ctx.enter_context(nc.psum_tensor(f"{name}_ps_kr{n}", [P, 512], F32)) for n in range(2)]
        ps_v = [ctx.enter_context(nc.psum_tensor(f"{name}_ps_v{n}", [P, 512], F32)) for n in range(2)]
        ps_t = [ctx.enter_context(nc.psum_tensor(f"{name}_ps_t{n}", [P, 512], F32)) for n in range(2)]

        s_id = sem("ident_made")
        s_w = sem("weights_loaded")
        s_x = [sem(f"x_loaded{n}") for n in range(NX)]
        s_wt = sem("weight_transposed")
        s_wc = sem("weight_copied")
        s_st = sem("ln_chain")
        s_ve = sem("variance_ready")
        s_rs = sem("rstd_ready")
        s_hx = sem("hx_ready")
        s_t = sem("transposed")
        s_tc = sem("xhT_ready")
        s_prev = sem("prev_column_ready")
        s_dsh = sem("dsh_ready")
        s_xk = sem("xk_ready")
        s_xr = sem("xr_ready")
        s_kr = sem("kr_in_psum")
        s_kre = sem("kr_evacuated")
        s_relu = sem("relu_done")
        s_v = sem("v_in_psum")
        s_vt = sem("v_used")
        s_x1 = sem("x1_ready")
        s_h2 = sem("h2_ready")
        s_xs = sem("xs_ready")
        s_t2 = sem("h2_transposed")
        s_t2c = sem("h2T_ready")
        s_pad = sem("pad_zeroed")
        s_out = sem("out_stored")
        s_ht = sem("hT_stored")
        block = ctx.enter_context(nc.Block())

        def over_chunks(eng, prologue, body):
            if prologue:
                prologue()
            with eng.Fori(0, BATCH - 1) as b:
                for c in range(FC):
                    body(b, c, FC * b + c, 0)
            for c in range(FC):
                body(BATCH - 1, c, FC * (BATCH - 1) + c, FC - c)


        @block.sync
        def _(sp):
            for n, w in enumerate((w_r, w_k, w_v)):
                sp.dma_start(w_nat[:, n], w.rearrange("(o p) c -> p o c", p=P)).then_inc(s_w, 16)
            for n, m in enumerate((mu_r, mu_k)):
                sp.dma_start(mu[:, n, :], m.rearrange("(o p) -> p o", p=P),
                             allow_slow_non_contiguous=True).then_inc(s_w, 16)
            for c in range(NX):
                sp.dma_start(x[:, c], x_v[c]).then_inc(s_x[c], 16)
            if mixer:
                sp.wait_ge(s_pad, 1)
                for b in range(BATCH):
                    sp.dma_start(hT_pad[:, :, b * ROW:b * ROW + PAD_L], zpad[:, :, 0:PAD_L],
                                 allow_slow_non_contiguous=True).then_inc(s_ht, 16)
                    sp.dma_start(hT_pad[:, :, (b + 1) * ROW - PAD_R:(b + 1) * ROW], zpad[:, :, 0:PAD_R]).then_inc(s_ht, 16)
                sp.dma_start(hT_pad[:, :, BATCH * ROW:], zpad[:, :, :]).then_inc(s_ht, 16)
            pads = (2 * BATCH + 1) * 16 if mixer else 0

            def body(b, c, i, left):
                sp.wait_ge(s_xs if mixer else s_x1, i + 1)
                sp.dma_start(out_v[i], x[:, c]).then_inc(s_out, 16)
                if left == 0:
                    sp.wait_ge(s_out, 16 * (i + 1))
                    sp.dma_start(x[:, c], x_v[i + NX]).then_inc(s_x[c], 16)
                if mixer:
                    sp.wait_ge(s_t2c, NB * (i + 1))
                    sp.dma_start(hT_pad[:, :, bass.ds(ROW * b + PAD_L + c * FT, FT)], h2T[:, :, :]).then_inc(s_ht, 16)

            over_chunks(sp, None, body)
            sp.wait_ge(s_out, 16 * BATCH * FC)
            if mixer:
                sp.wait_ge(s_ht, pads + 16 * BATCH * FC)

        @block.gpsimd
        def _(pool):
            nc.gpsimd.memset(ident[:, :], 0.0).then_inc(s_id, 1)
            nc.gpsimd.memset(half[:, :], -0.5).then_inc(s_id, 1)
            pool.wait_ge(s_id, 2)
            nc.gpsimd.affine_select(out=ident[:, :], in_=ident[:, :], compare_op=ALU.not_equal, fill=1.0,
                                    base=0, pattern=[[-1, P]], channel_multiplier=1).then_inc(s_id, 1)
            if mixer:
                nc.gpsimd.memset(zpad[:, :, :], 0.0).then_inc(s_pad, 1)
            norms = 2 if mixer else 1

            def power(which, k):
                pool.wait_ge(s_ve, k + 1)
                nc.gpsimd.tensor_tensor(rstd[:, which], ve[:, which], half[:, :], ALU.pow).then_inc(s_rs, 1)

            def shift(i, slot):
                pool.wait_ge(s_tc, NB * (i + 1))
                pool.wait_ge(s_prev, i + 1)
                if not (isinstance(i, int) and i == 0):
                    pool.wait_ge(s_xr, NB * i)
                nc.gpsimd.tensor_tensor(dsh[:, :, :], xhT[:, slot, :, 1:FT + 1], xhT[:, slot, :, 0:FT],
                                        ALU.subtract).then_inc(s_dsh, 1)

            def prologue():
                power(0, 0)
                shift(0, 0)
                power(0, 1)
                shift(1, 1)

            def body(b, c, i, left):
                if mixer:
                    power(1, 2 * i + 2 - (1 if left == 1 else 0))
                    pool.wait_ge(s_h2, FJ * (i + 1))
                    nc.gpsimd.tensor_tensor(x[:, c], x[:, c], h2[:, :, :], ALU.add).then_inc(s_xs, 1)
                if left == 0 or left > 2:
                    power(0, (2 * i + 3) if mixer else i + 2)
                    shift(i + 2, c % 2)

            over_chunks(pool, prologue, body)

        @block.scalar
        def _(act):
            def copy_weights():
                for g in range(3 * NB):
                    act.wait_ge(s_wt, g + 1)
                    nc.scalar.activation(wT[:, g // NB, g % NB, :], ps_t[g % 2][:, :], ACT.Copy).then_inc(s_wc, 1)

            def copy_xhT(i, slot, seq_start):
                if not (isinstance(i, int) and i < 2):
                    act.wait_ge(s_xr, NB * (i - 1))
                if seq_start:
                    nc.scalar.activation(xhT[:, slot, :, 0], ident[:, 0:NB], ACT.Copy, scale=0.0).then_inc(s_prev, 1)
                else:
                    act.wait_ge(s_tc, NB * i)
                    nc.scalar.activation(xhT[:, slot, :, 0], xhT[:, 1 - slot, :, FT], ACT.Copy).then_inc(s_prev, 1)
                for f in range(NB):
                    act.wait_ge(s_t, NB * i + f + 1)
                    nc.scalar.activation(xhT[:, slot, f, 1:FT + 1], ps_t[f % 2][:, :], ACT.Copy).then_inc(s_tc, 1)

            def copy_k(i):
                for d in range(NB):
                    act.wait_ge(s_kr, 2 * NB * i + d + 1)
                    nc.scalar.activation(ka[:, d, :], ps_kr[d % 2][:, :], ACT.Relu).then_inc(s_kre, 1)
                    act.wait_ge(s_kre, 2 * NB * i + d + 1)
                    nc.scalar.activation(ka[:, d, :], ka[:, d, :], ACT.Square).then_inc(s_relu, 1)

            def copy_r(i):
                if not (isinstance(i, int) and i == 0):
                    act.wait_ge(s_x1, i)
                for j in range(FJ):
                    act.wait_ge(s_kr, 2 * NB * i + NB + j + 1)
                    nc.scalar.activation(rt[:, j, :], ps_kr[j % 2][:, :], ACT.Tanh, scale=0.5).then_inc(s_kre, 1)

            def prologue():
                act.wait_ge(s_id, 3)
                copy_weights()
                copy_xhT(0, 0, True)
                copy_k(0)
                copy_r(0)
                copy_xhT(1, 1, False)

            def body(b, c, i, left):
                if left == 0 or left > 1:
                    copy_k(i + 1)
                if mixer:
                    act.wait_ge(s_ht, (2 * BATCH + 1) * 16 + 16 * i)
                    for f in range(NB):
                        act.wait_ge(s_t2, NB * i + f + 1)
                        nc.scalar.activation(h2T[:, f, :], ps_t[f % 2][:, :], ACT.Copy).then_inc(s_t2c, 1)
                if left == 0 or left > 1:
                    copy_r(i + 1)
                if left == 0 or left > 2:
                    copy_xhT(i + 2, c % 2, c + 2 == FC)

            over_chunks(act, prologue, body)

        @block.vector
        def _(dve):
            V = nc.vector
            def norm(which, src, dst, st, k, done, before):
                for j in range(FJ):
                    V.bn_stats(out=stats[:, j, :], in_=src[:, j, :]).then_inc(s_st, 1)
                dve.wait_ge(s_st, st + FJ)
                V.memset(mark[:, :], 0.0)
                for j in range(FJ):
                    V.bn_aggr(out=mv[:, which, j, :], in_=stats[:, j, :]).then_inc(s_st, 1)
                dve.wait_ge(s_st, st + 2 * FJ)
                V.tensor_scalar(ve[:, which], mv[:, which, :, 1], EPS, None, ALU.add).then_inc(s_ve, 1)
                dve.wait_ge(s_rs, k + 1)
                before()
                for j in range(FJ):
                    V.tensor_scalar(dst[:, j, :], src[:, j, :], mv[:, which, j, 0:1], rstd[:, which, j:j + 1],
                                    ALU.subtract, ALU.mult).then_inc(done, 1)

            per = 4 * FJ if mixer else 2 * FJ

            def norm1(i, slot, st, k, nth):
                dve.wait_ge(s_x[slot], 16 * nth)

                def free():
                    if not (isinstance(i, int) and i == 0):
                        dve.wait_ge(s_t, NB * i)
                norm(0, x[:, slot], hx, st, k, s_hx, free)

            def mixes(i, slot):
                dve.wait_ge(s_dsh, i + 1)
                for n, (dst, done) in ((1, (xk, s_xk)), (0, (xr, s_xr))):
                    for f in range(NB):
                        V.scalar_tensor_tensor(out=dst[:, f, :], in0=dsh[:, f, :], scalar=mu[:, n, f:f + 1],
                                               in1=xhT[:, slot, f, 0:FT], op0=ALU.mult, op1=ALU.add).then_inc(done, 1)

            dve.wait_ge(s_w, 5 * 16)
            norm1(0, 0, 0, 0, 1)
            mixes(0, 0)
            norm1(1, 1, 2 * FJ, 1, 1)
            mixes(1, 1)

            def body(b, c, i, left):
                for j in range(FJ):
                    dve.wait_ge(s_v, FJ * i + j + 1)
                    dve.wait_ge(s_kre, 2 * NB * i + NB + j + 1)
                    V.scalar_tensor_tensor(out=rt[:, j, :], in0=rt[:, j, :], scalar=1.0, in1=ps_v[j % 2][:, :],
                                           op0=ALU.add, op1=ALU.mult).then_inc(s_vt, 1)
                dve.wait_ge(s_vt, FJ * (i + 1))
                for j in range(FJ):
                    ins = V.scalar_tensor_tensor(out=x[:, c, j, :], in0=rt[:, j, :], scalar=0.25,
                                                 in1=x[:, c, j, :], op0=ALU.mult, op1=ALU.add)
                ins.then_inc(s_x1, 1)
                if mixer:
                    dve.wait_ge(s_x1, i + 1)

                    def free():
                        if left == 1:
                            dve.wait_ge(s_t2, NB * i)
                            dve.wait_ge(s_xs, i)
                    last = 1 if left == 1 else 0
                    norm(1, x[:, c], h2, per * i + 4 * FJ - 2 * FJ * last, 2 * i + 2 - last, s_h2, free)
                if left == 0 or left > 2:
                    c2 = (c + 2) % NX
                    nth = (b if c + 2 < FC else b + 1) + 1
                    norm1(i + 2, c2, per * i + (6 * FJ if mixer else 4 * FJ), (2 * i + 3) if mixer else i + 2, nth)
                    mixes(i + 2, c % 2)

            over_chunks(dve, None, body)

        @block.tensor
        def _(pe):
            M = nc.tensor

            def turn_weights():
                for g in range(3 * NB):
                    if g >= 2:
                        pe.wait_ge(s_wc, g - 1)
                    for o in range(NB):
                        ins = M.transpose(ps_t[g % 2][:, o * P:(o + 1) * P],
                                          w_nat[:, g // NB, o, (g % NB) * P:(g % NB + 1) * P], ident[:, :])
                    ins.then_inc(s_wt, 1)

            def turn(i, src, ready, done, copied_before):
                pe.wait_ge(ready, FJ * (i + 1))
                for f in range(NB):
                    copied_before(f)
                    for j in range(FJ):
                        ins = M.transpose(ps_t[f % 2][:, j * P:(j + 1) * P], src[:, j, f * P:(f + 1) * P], ident[:, :])
                    ins.then_inc(done, 1)

            def turn1(i):
                def bank(f):
                    if f >= 2:
                        pe.wait_ge(s_tc, NB * i + f - 1)
                    elif mixer and not (isinstance(i, int) and i < 2):
                        pe.wait_ge(s_t2c, NB * (i - 1))
                    elif isinstance(i, int) and i == 0:
                        pe.wait_ge(s_wc, 3 * NB)
                    else:
                        pe.wait_ge(s_tc, NB * i)
                turn(i, hx, s_hx, s_t, bank)

            def turn2(i):
                def bank(f):
                    if f >= 2:
                        pe.wait_ge(s_t2c, NB * i + f - 1)
                    elif isinstance(i, int) and i == BATCH * FC - 1:
                        pe.wait_ge(s_tc, NB * BATCH * FC)
                    else:
                        pe.wait_ge(s_tc, NB * (i + 2))
                turn(i, h2, s_h2, s_t2, bank)

            def bank_free(n, first):
                if not (first and n < 2):
                    pe.wait_ge(s_kre, n - 1)

            def k_products(i):
                pe.wait_ge(s_xk, NB * (i + 1))
                for d in range(NB):
                    bank_free(2 * NB * i + d, isinstance(i, int) and i == 0 and d < 2)
                    for f in range(NB):
                        ins = M.matmul(ps_kr[d % 2][:, :], wT[:, 1, f, d * P:(d + 1) * P], xk[:, f, :],
                                       start=(f == 0), stop=(f == NB - 1))
                    ins.then_inc(s_kr, 1)

            def r_products(i):
                pe.wait_ge(s_xr, NB * (i + 1))
                for j in range(FJ):
                    bank_free(2 * NB * i + NB + j, False)
                    for f in range(NB):
                        ins = M.matmul(ps_kr[j % 2][:, :], xr[:, f, j * P:(j + 1) * P], wT[:, 0, f, :],
                                       start=(f == 0), stop=(f == NB - 1))
                    ins.then_inc(s_kr, 1)

            def v_products(i, c):
                pe.wait_ge(s_relu, NB * (i + 1))
                for j in range(FJ):
                    if j >= 2 or not (c == 0):
                        pe.wait_ge(s_vt, FJ * i + (j - 1 if j >= 2 else 0))
                    for d in range(NB):
                        ins = M.matmul(ps_v[j % 2][:, :], ka[:, d, j * P:(j + 1) * P], wT[:, 2, d, :],
                                       start=(d == 0), stop=(d == NB - 1))
                    ins.then_inc(s_v, 1)

            def prologue():
                pe.wait_ge(s_id, 3)
                pe.wait_ge(s_w, 5 * 16)
                turn_weights()
                turn1(0)
                k_products(0)
                r_products(0)
                turn1(1)

            def body(b, c, i, left):
                v_products(i, c)
                if left == 0 or left > 1:
                    k_products(i + 1)
                if mixer:
                    turn2(i)
                if left == 0 or left > 1:
                    r_products(i + 1)
                if left == 0 or left > 2:
                    turn1(i + 2)

            over_chunks(pe, prologue, body)


def bcast(ap, n):
    return ap.unsqueeze(1).to_broadcast([ap.shape[0], n, ap.shape[1]])


def mixer_phase(nc, hT_pad, xs_in, w_in, conv_w, conv_b, w_x, w_dt, b_dt, w_out, a_mat, d_vec, bc_dram, out):
    xs_v = xs_in.rearrange("b (c j p) d -> (b c) p j d", c=MC, p=P)
    out_v = out.rearrange("b (c j p) d -> (b c) p j d", c=MC, p=P)
    LAST = BATCH * MC - 1

    with ExitStack() as ctx:
        def sb(n, shape):
            return ctx.enter_context(nc.sbuf_tensor(f"mx_{n}", shape, F32))

        def sem(n):
            return ctx.enter_context(nc.semaphore(f"mx_{n}"))

        ident = sb("ident", [P, P])
        w_in_sb = sb("w_in", [P, NB, 2 * DI])
        w_x_sb = sb("w_x", [P, ND, 2 * DS])
        w_dt_sb = sb("w_dt", [P, ND, DI])
        w_out_sb = sb("w_out", [P, ND, DM])
        cw = sb("cw", [P, KC, ND])
        cb = sb("cb", [P, ND])
        bdt = sb("bdt", [P, ND])
        a_sb = sb("a", [P, ND, DS])
        d_sb = sb("d", [P, ND])
        hst = sb("hst", [P, ND, DS])
        hT = sb("hT", [P, 2, NB, TH])
        u = sb("u", [P, 2, ND, T])
        dl = sb("dl", [P, 2, ND, T])
        du = sb("du", [P, ND, T])
        ex = sb("ex", [P, ND, T])
        zs = sb("zs", [P, ND, T])
        bs = sb("bs", [P, NG, SG, T])
        cs = sb("cs", [P, NG, SG, T])
        bc = sb("bc", [2 * DS, T])
        dbu = sb("dbu", [P, 2, SG, T])
        hp = sb("hp", [P, NH, SG, T])
        xo = sb("xo", [P, TJ, DM])

        ps_y = ctx.enter_context(nc.psum_tensor("mx_ps_y", [P, ND, T], F32))
        ps_da = [ctx.enter_context(nc.psum_tensor(f"mx_ps_da{n}", [P, 2, T], F32)) for n in range(2)]
        ps_m = [ctx.enter_context(nc.psum_tensor(f"mx_ps_m{n}", [P, 512], F32)) for n in range(2)]

        s_id = sem("ident_made")
        s_w = sem("weights_loaded")
        s_mean = sem("w_in_mean")
        s_cen = sem("w_in_centred")
        s_prep = sem("weights_scaled")
        s_ht = [sem(f"hT_loaded{n}") for n in range(2)]
        s_pi = sem("input_in_psum")
        s_pz = sem("gate_in_psum")
        s_pb = sem("bc_in_psum")
        s_pd = sem("dt_in_psum")
        s_po = sem("out_in_psum")
        s_cv = sem("conv_steps")
        s_cq = sem("conv_ready")
        s_ct = sem("conv_tanh")
        s_u = sem("u_ready")
        s_bc = sem("bc_copied")
        s_bcd = sem("bc_stored")
        s_bl = [sem(f"b_loaded{n}") for n in range(NG)]
        s_cl = [sem(f"c_loaded{n}") for n in range(NG)]
        s_rl = sem("dt_clipped")
        s_ab = sem("dt_abs")
        s_sp = sem("softplus_steps")
        s_dl = sem("delta_ready")
        s_du = sem("du_ready")
        s_m1 = sem("dbu_ready")
        s_da = sem("da_ready")
        s_sc = sem("scanned")
        s_m2 = sem("hc_ready")
        s_pr = sem("pairs_added")
        s_r = sem("states_summed")
        s_st = sem("state_kept")
        s_zt = sem("z_tanh")
        s_zs = sem("zs_ready")
        s_yd = sem("yd_ready")
        s_g = sem("gated")
        s_x = sem("xs_loaded")
        s_o = sem("out_ready")
        s_out = sem("out_stored")
        s_rst = sem("state_zeroed")
        block = ctx.enter_context(nc.Block())

        mean_w = hp[:, 0, 0, 0:P]

        IN_AT = {6 + b: b for b in range(ND)}
        GATE_AT = {14: (0, 1), 15: (2, 3), 16: (4, 5), 20: (6,), 23: (7,)}
        BC_AT = 17
        DT_AT = {n: b for b, n in enumerate((18, 19, 21, 22, 24, 25, 27, 28))}
        OUT_AT = {31: (0, 1), NU: (2, 3), NU + 2: (4, 5), NU + 4: (6, 7)}
        YG_AT = {29: 0, 31: 1, NU + 1: 2, NU + 3: 3}
        EVAC_AT = 5
        LN_AT, ADD_AT = 30, 31
        PAIR_LAG, SUM_LAG = 2, 3
        order = []
        for n in range(NU):
            if n in IN_AT:
                order.append(("in", IN_AT[n]))
            order += [("gate", b) for b in GATE_AT.get(n, ())]
            if n == BC_AT:
                order.append(("bc", 0))
            if n in DT_AT:
                order.append(("dt", DT_AT[n]))
        order += [("out", 0), ("out", 1)]
        first_order = [("in", b) for b in range(ND)] + [("bc", 0)] + [("dt", b) for b in range(ND)]

        def bank(kind, b, i, par, first=False):
            if first:
                return ps_m[first_order.index((kind, b)) % 2]
            return ps_m[(len(first_order) + len(order) * par + order.index((kind, b))) % 2]

        def over_chunks(eng, prologue, body, sequence=None, epilogue=None):
            if prologue:
                prologue()
            if sequence:
                sequence(0)
            body(0, 0)
            body(1, 1)
            with eng.Fori(1, MC // 2) as c2:
                for par in range(2):
                    body(2 * c2 + par, par)
            with eng.Fori(1, BATCH) as b:
                if sequence:
                    sequence(b)
                with eng.Fori(0, MC // 2) as c2:
                    for par in range(2):
                        body(MC * b + 2 * c2 + par, par)
            if epilogue:
                epilogue()

        def is0(i):
            return isinstance(i, int) and i == 0

        @block.sync
        def _(sp):
            for dst, src in (
                (w_in_sb[:, :, :], w_in.rearrange("(f p) n -> p f n", p=P)),
                (w_dt_sb[:, :, :], w_dt.rearrange("(f p) n -> p f n", p=P)),
                (w_out_sb[:, :, :], w_out.rearrange("(f p) n -> p f n", p=P)),
                (w_x_sb[:, :, :], w_x.rearrange("(f p) n -> p f n", p=P)),
                (a_sb[:, :, :], a_mat.rearrange("(f p) n -> p f n", p=P)),
                (cw[:, :, :], conv_w.rearrange("k o (f p) -> p (k o) f", p=P)),
                (cb[:, :], conv_b.rearrange("(f p) -> p f", p=P)),
                (bdt[:, :], b_dt.rearrange("(f p) -> p f", p=P)),
                (d_sb[:, :], d_vec.rearrange("(f p) -> p f", p=P)),
            ):
                sp.dma_start(dst, src, allow_slow_non_contiguous=True).then_inc(s_w, 16)

            def load_hT(b, c, par):
                sp.dma_start(hT[:, par], hT_pad[:, :, bass.ds(ROW * b + T * c, TH)]).then_inc(s_ht[par], 16)

            def load_bc(i, units, between=None):
                sp.wait_ge(s_bc, i + 1)
                if units is not None:
                    for g in range(NG):
                        sp.wait_ge(s_bl[g], 16 * i)
                        sp.wait_ge(s_cl[g], 16 * i)
                sp.dma_start(bc_dram[:, :], bc[:, :]).then_inc(s_bcd, 16)
                sp.wait_ge(s_bcd, 16 * (i + 1))
                for g in range(NG):
                    for dst, done, first, used in ((bs, s_bl, 0, s_m1), (cs, s_cl, DS, s_m2)):
                        if units is not None:
                            sp.wait_ge(used, units + ND * (g + 1))
                        rows = bc_dram[first + SG * g:first + SG * (g + 1), :].rearrange("s t -> (s t)")
                        sp.dma_start(dst[:, g].rearrange("p s t -> p (s t)"),
                                     rows.unsqueeze(0).to_broadcast([P, SG * T])).then_inc(done[g], 16)
                    if g == NG - 2 and between:
                        between()

            def chunk(i, par, b_next, c_next):
                if not is0(i):
                    sp.wait_ge(s_out, 16 * i)
                sp.dma_start(xo[:, :, :], xs_v[i]).then_inc(s_x, 16)

                def columns():
                    sp.wait_ge(s_zs, ND * (i + 1))
                    load_hT(b_next, c_next, par)
                load_bc(i + 1, NU * i, columns)
                sp.wait_ge(s_o, i + 1)
                sp.dma_start(out_v[i], xo[:, :, :]).then_inc(s_out, 16)

            load_hT(0, 0, 0)
            load_hT(0, 1, 1)
            load_bc(0, None)
            def last_pair(b):
                for par in range(2):
                    chunk(MC * b + MC - 2 + par, par, b + 1, par)

            for par in range(2):
                chunk(par, par, 0, 2 + par)
            with sp.Fori(1, MC // 2 - 1) as c2:
                for par in range(2):
                    chunk(2 * c2 + par, par, 0, 2 * c2 + 2 + par)
            last_pair(0)
            with sp.Fori(1, BATCH) as b:
                with sp.Fori(0, MC // 2 - 1) as c2:
                    for par in range(2):
                        chunk(MC * b + 2 * c2 + par, par, b, 2 * c2 + 2 + par)
                last_pair(b)
            sp.wait_ge(s_out, 16 * (LAST + 1))

        @block.gpsimd
        def _(pool):
            G = nc.gpsimd
            G.memset(ident[:, :], 0.0).then_inc(s_id, 1)
            G.memset(mean_w, 1.0 / DM).then_inc(s_id, 1)
            pool.wait_ge(s_id, 2)
            G.affine_select(out=ident[:, :], in_=ident[:, :], compare_op=ALU.not_equal, fill=1.0,
                            base=0, pattern=[[-1, P]], channel_multiplier=1).then_inc(s_id, 1)

            def add_log(i, slot, half):
                pool.wait_ge(s_sp, (ND + 1) * (i + 1))
                h = slice(half * ND // 2, (half + 1) * ND // 2)
                G.tensor_tensor(dl[:, slot, h, :], dl[:, slot, h, :], ex[:, h, :], ALU.add).then_inc(s_dl, 1)

            def pairs(i, n):
                k = n % NH
                pool.wait_ge(s_m2, NU * i + n + 1)
                G.tensor_tensor(hp[:, k, 0:2, :], hp[:, k, 0:2, :], hp[:, k, 2:4, :], ALU.add).then_inc(s_pr, 1)

            def body(i, par):
                for n in range(NU):
                    g, b = divmod(n, ND)
                    if n == 0:
                        pool.wait_ge(s_dl, 2 * (i + 1))
                    if g == 0:
                        G.tensor_tensor(du[:, b, :], dl[:, par, b, :], u[:, par, b, :], ALU.mult).then_inc(s_du, 1)
                    if b == 0:
                        pool.wait_ge(s_bl[g], 16 * (i + 1))
                    if g == 0:
                        pool.wait_ge(s_du, ND * i + b + 1)
                    if not (is0(i) and n < 2):
                        pool.wait_ge(s_sc, 2 * NU * i + 2 * (n - 1))
                    G.tensor_tensor(dbu[:, n % 2], bs[:, g], bcast(du[:, b, :], SG), ALU.mult).then_inc(s_m1, 1)
                    if n >= PAIR_LAG:
                        pairs(i, n - PAIR_LAG)
                    elif not is0(i):
                        pairs(i - 1, NU + n - PAIR_LAG)
                    if n == ADD_AT:
                        for half in range(2):
                            add_log(i + 1, 1 - par, half)

            over_chunks(pool, lambda: [add_log(0, 0, h) for h in range(2)], body, None, lambda: [pairs(LAST, n) for n in range(NU - PAIR_LAG, NU)])

        @block.scalar
        def _(act):
            A = nc.scalar

            def conv_tanh(i, b):
                act.wait_ge(s_cq, ND * i + b + 1)
                A.activation(ex[:, b, :], u_of(i)[:, b, :], ACT.Tanh).then_inc(s_ct, 1)

            slots = {}

            def u_of(i):
                return u[:, slots["next"]]

            def copy_bc(i, par, first=False):
                act.wait_ge(s_pb, i + 1)
                if not is0(i):
                    act.wait_ge(s_bcd, 16 * i)
                A.activation(bc[:, :], bank("bc", 0, i, par, first)[0:2 * DS, 0:T], ACT.Copy).then_inc(s_bc, 1)

            def exp_neg(i, b, ps):
                act.wait_ge(s_rl, ND * i + b + 1)
                A.activation(ex[:, b, :], ps[:, 0:T], ACT.Abs, bias=bdt[:, b:b + 1]).then_inc(s_ab, 1)
                act.wait_ge(s_ab, ND * i + b + 1)
                A.activation(ex[:, b, :], ex[:, b, :], ACT.Exp, scale=-1.0).then_inc(s_sp, 1)

            def log(i):
                act.wait_ge(s_sp, (ND + 1) * i + ND)
                A.activation(ex[:, :, :], ex[:, :, :], ACT.Ln, bias=1.0).then_inc(s_sp, 1)

            def gate_tanh(i, par, b):
                act.wait_ge(s_pz, ND * i + b + 1)
                A.activation(zs[:, b, :], bank("gate", b, i, par)[:, 0:T], ACT.Tanh, scale=0.5).then_inc(s_zt, 1)

            def prologue():
                slots["next"] = 0
                for b in range(ND):
                    conv_tanh(0, b)
                copy_bc(0, 0, True)
                for b in range(ND):
                    exp_neg(0, b, bank("dt", b, 0, 0, True))
                log(0)

            def body(i, par):
                slots["next"] = 1 - par
                for n in range(NU):
                    g, b = divmod(n, ND)
                    if n == 0:
                        act.wait_ge(s_dl, 2 * (i + 1))
                    for half in range(2):
                        if not (is0(i) and n == 0):
                            act.wait_ge(s_sc, 2 * NU * i + 2 * n - 1 + half + (1 if n == 0 and half == 0 else 0))
                        for k in range(2):
                            s = SG * g + 2 * half + k
                            ins = A.activation(ps_da[half][:, k, :], dl[:, par, b, :], ACT.Exp, scale=a_sb[:, b, s:s + 1])
                        ins.then_inc(s_da, 1)
                    if n - 2 in IN_AT:
                        conv_tanh(i + 1, IN_AT[n - 2])
                    if n - 1 == BC_AT:
                        copy_bc(i + 1, par)
                    for bb in GATE_AT.get(n - 1, ()):
                        gate_tanh(i, par, bb)
                    if n - 2 in DT_AT:
                        exp_neg(i + 1, DT_AT[n - 2], bank("dt", DT_AT[n - 2], i, par))
                    if n == LN_AT:
                        log(i + 1)

            act.wait_ge(s_w, 16 * 9)
            over_chunks(act, prologue, body)

        @block.vector
        def _(dve):
            V = nc.vector

            def weights():
                dve.wait_ge(s_w, 16 * 9)
                V.tensor_scalar(cw[:, :, :], cw[:, :, :], 0.5, None, ALU.mult).then_inc(s_prep, 1)
                V.tensor_scalar(cb[:, :], cb[:, :], 0.5, None, ALU.mult).then_inc(s_prep, 1)
                V.tensor_scalar(w_out_sb[:, :, :], w_out_sb[:, :, :], 0.5, None, ALU.mult).then_inc(s_prep, 1)
                for c in range(2 * DI // 512):
                    dve.wait_ge(s_mean, c + 1)
                    for f in range(NB):
                        w = w_in_sb[:, f, 512 * c:512 * (c + 1)]
                        ins = V.tensor_tensor(w, w, ps_m[c % 2][:, :], ALU.subtract)
                    ins.then_inc(s_cen, 1)
                dve.wait_ge(s_prep, 3)

            def conv(i, b, step, slot, ps):
                q = u[:, slot, b, :]
                if step == 0:
                    dve.wait_ge(s_pi, ND * i + b + 1)
                    V.tensor_scalar(q, ps[:, 0:T], cw[:, 0, b:b + 1], cb[:, b:b + 1], ALU.mult, ALU.add).then_inc(s_cv, 1)
                else:
                    dve.wait_ge(s_cv, (KC - 1) * (ND * i + b) + step)
                    V.scalar_tensor_tensor(out=q, in0=ps[:, step:step + T], scalar=cw[:, step, b:b + 1], in1=q,
                                           op0=ALU.mult, op1=ALU.add).then_inc(s_cq if step == KC - 1 else s_cv, 1)

            def silu(i, b, slot):
                dve.wait_ge(s_ct, ND * i + b + 1)
                q = u[:, slot, b, :]
                V.scalar_tensor_tensor(out=q, in0=ex[:, b, :], scalar=1.0, in1=q, op0=ALU.add, op1=ALU.mult).then_inc(s_u, 1)

            def split_dt(i, b, slot, ps):
                dve.wait_ge(s_pd, ND * i + b + 1)
                V.tensor_scalar(dl[:, slot, b, :], ps[:, 0:T], bdt[:, b:b + 1], 0.0, ALU.add, ALU.max).then_inc(s_rl, 1)

            def gate(i, b, ps):
                dve.wait_ge(s_zt, ND * i + b + 1)
                V.scalar_tensor_tensor(out=zs[:, b, :], in0=zs[:, b, :], scalar=1.0, in1=ps[:, 0:T],
                                       op0=ALU.add, op1=ALU.mult).then_inc(s_zs, 1)

            def gated(i, j, slot):
                dve.wait_ge(s_r, NU * i + NU - ND + 2 * j + 2)
                for b in (2 * j, 2 * j + 1):
                    V.scalar_tensor_tensor(out=u[:, slot, b, :], in0=u[:, slot, b, :], scalar=d_sb[:, b:b + 1],
                                           in1=ps_y[:, b, :], op0=ALU.mult, op1=ALU.add).then_inc(s_yd, 1)
                dve.wait_ge(s_yd, ND * i + 2 * j + 2)
                dve.wait_ge(s_zs, ND * (i + 1))
                for b in (2 * j, 2 * j + 1):
                    V.tensor_tensor(u[:, slot, b, :], u[:, slot, b, :], zs[:, b, :], ALU.mult).then_inc(s_g, 1)

            def residual(i, par):
                dve.wait_ge(s_po, i + 1)
                dve.wait_ge(s_x, 16 * (i + 1))
                for j in range(TJ):
                    ins = V.tensor_tensor(xo[:, j, :], bank("out", j, i, par)[:, :], xo[:, j, :], ALU.add)
                ins.then_inc(s_o, 1)

            def keep(i, n):
                g, b = divmod(n, ND)
                dve.wait_ge(s_sc, 2 * (NU * i + n + 1))
                V.tensor_copy(hst[:, b, SG * g:SG * (g + 1)], hp[:, n % NH, :, T - 1]).then_inc(s_st, 1)

            def times_c(i, n):
                g, b = divmod(n, ND)
                if b == 0:
                    dve.wait_ge(s_cl[g], 16 * (i + 1))
                h = hp[:, n % NH]
                dve.wait_ge(s_st, NU * i + n + 1)
                V.tensor_tensor(h, h, cs[:, g], ALU.mult).then_inc(s_m2, 1)

            def scans(i, n, half):
                g, b = divmod(n, ND)
                dve.wait_ge(s_da, 2 * (NU * i + n) + half + 1)
                for k in range(2):
                    s = 2 * half + k
                    ins = V.tensor_tensor_scan(hp[:, n % NH, s, :], ps_da[half][:, k, :], dbu[:, n % 2, s, :],
                                               hst[:, b, SG * g + s:SG * g + s + 1], ALU.mult, ALU.add)
                ins.then_inc(s_sc, 1)

            def prologue():
                weights()
                for b in range(ND):
                    for step in range(KC):
                        conv(0, b, step, 0, bank("in", b, 0, 0, True))
                    silu(0, b, 0)
                for b in range(ND):
                    split_dt(0, b, 0, bank("dt", b, 0, 0, True))

            seq = {}

            def sequence(b):
                if not is0(b):
                    dve.wait_ge(s_st, NU * MC * b)
                V.memset(hst[:, :, :], 0.0).then_inc(s_rst, 1)
                seq["now"] = b

            def body(i, par):
                nxt = 1 - par
                for n in range(NU):
                    g, b = divmod(n, ND)
                    steps = [lambda s=s: conv(i + 1, IN_AT[n - 1], s, nxt, bank("in", IN_AT[n - 1], i, par))
                             for s in range(KC)] if n - 1 in IN_AT else [lambda: None] * KC
                    if n == 0:
                        if not is0(i):
                            dve.wait_ge(s_st, NU * i)
                        dve.wait_ge(s_rst, seq["now"] + 1)
                    dve.wait_ge(s_m1, NU * i + n + 1)
                    if not (is0(i) and n < NH):
                        dve.wait_ge(s_r, NU * i + n - NH + 1)
                    steps[0]()
                    scans(i, n, 0)
                    steps[1]()
                    if n > 0:
                        keep(i, n - 1)
                    steps[2]()
                    scans(i, n, 1)
                    if n > 0:
                        times_c(i, n - 1)
                    elif not is0(i):
                        times_c(i - 1, NU - 1)
                    steps[3]()
                    if n - 2 in IN_AT:
                        silu(i + 1, IN_AT[n - 2], nxt)
                    for bb in GATE_AT.get(n - 1, ()):
                        gate(i, bb, bank("gate", bb, i, par))
                    if n - 1 in DT_AT:
                        split_dt(i + 1, DT_AT[n - 1], nxt, bank("dt", DT_AT[n - 1], i, par))
                    if n in YG_AT:
                        gated(i, YG_AT[n], par)
                    if n + NU in YG_AT and not is0(i):
                        gated(i - 1, YG_AT[n + NU], nxt)
                    if n == EVAC_AT and not is0(i):
                        residual(i - 1, nxt)
                keep(i, NU - 1)

            def epilogue():
                times_c(LAST, NU - 1)
                for n in sorted(YG_AT):
                    if n >= NU:
                        gated(LAST, YG_AT[n], LAST % 2)
                residual(LAST, LAST % 2)

            over_chunks(dve, prologue, body, sequence, epilogue)

        @block.tensor
        def _(pe):
            M = nc.tensor

            def evacuated(kind, b, i):
                if kind == "in":
                    pe.wait_ge(s_cq, ND * (i + 1) + b + 1)
                elif kind == "bc":
                    pe.wait_ge(s_bc, i + 2)
                elif kind == "dt":
                    pe.wait_ge(s_ab, ND * (i + 1) + b + 1)
                elif kind == "gate":
                    pe.wait_ge(s_zs, ND * i + b + 1)
                else:
                    pe.wait_ge(s_o, i + 1)

            def bank_free(kind, b, i, first):
                if first:
                    at = first_order.index((kind, b))
                    if at >= 2:
                        evacuated(*first_order[at - 2], -1)
                    else:
                        pe.wait_ge(s_cen, 2 * DI // 512)
                    return
                at = order.index((kind, b))
                if at >= 2:
                    evacuated(*order[at - 2], i)
                elif is0(i):
                    evacuated(*first_order[at - 2], -1)
                else:
                    evacuated(*order[at - 2], i - 1)

            def input_product(i, b, par, first=False):
                bank_free("in", b, i - 1, first)
                if b == 0:
                    pe.wait_ge(s_ht[i_par(i, par, first)], 16 if first else 8 * (i - (1 - par)) + 16)
                ps = bank("in", b, i - 1, par, first)
                for f in range(NB):
                    ins = M.matmul(ps[:, 0:TH], w_in_sb[:, f, b * P:(b + 1) * P], hT[:, i_par(i, par, first), f, :],
                                   start=(f == 0), stop=(f == NB - 1))
                ins.then_inc(s_pi, 1)

            def i_par(i, par, first):
                return 0 if first else 1 - par

            def gate_product(i, b, par):
                bank_free("gate", b, i, False)
                ps = bank("gate", b, i, par)
                for f in range(NB):
                    ins = M.matmul(ps[:, 0:T], w_in_sb[:, f, DI + b * P:DI + (b + 1) * P], hT[:, par, f, PAD_L:PAD_L + T],
                                   start=(f == 0), stop=(f == NB - 1))
                ins.then_inc(s_pz, 1)

            def bc_product(i, par, first=False):
                slot = 0 if first else 1 - par
                bank_free("bc", 0, i - 1, first)
                pe.wait_ge(s_u, ND * (i + 1))
                for k in range(ND):
                    ins = M.matmul(bank("bc", 0, i - 1, par, first)[0:2 * DS, 0:T], w_x_sb[:, k, :], u[:, slot, k, :],
                                   start=(k == 0), stop=(k == ND - 1))
                ins.then_inc(s_pb, 1)

            def dt_product(i, b, par, first=False):
                slot = 0 if first else 1 - par
                bank_free("dt", b, i - 1, first)
                for k in range(ND):
                    ins = M.matmul(bank("dt", b, i - 1, par, first)[:, 0:T], w_dt_sb[:, k, b * P:(b + 1) * P],
                                   u[:, slot, k, :], start=(k == 0), stop=(k == ND - 1))
                ins.then_inc(s_pd, 1)

            def out_product(i, blocks, slot, par):
                for b in blocks:
                    pe.wait_ge(s_g, ND * i + b + 1)
                    for j in range(TJ):
                        if b == 0:
                            bank_free("out", j, i, False)
                        ins = M.matmul(bank("out", j, i, par)[:, :], u[:, slot, b, j * P:(j + 1) * P], w_out_sb[:, b, :],
                                       start=(b == 0), stop=(b == ND - 1))
                if blocks[-1] == ND - 1:
                    ins.then_inc(s_po, 1)

            def sum_states(i, n):
                g, b = divmod(n, ND)
                pe.wait_ge(s_pr, NU * i + n + 1)
                for k in range(SG // 2):
                    ins = M.matmul(ps_y[:, b, :], ident[:, :], hp[:, n % NH, k, :],
                                   start=(g == 0 and b % 2 == 0 and k == 0), stop=(g == NG - 1 and k == SG // 2 - 1),
                                   skip_group_check=True)
                ins.then_inc(s_r, 1)

            def prologue():
                pe.wait_ge(s_id, 3)
                pe.wait_ge(s_w, 16 * 9)
                for c in range(2 * DI // 512):
                    if c >= 2:
                        pe.wait_ge(s_cen, c - 1)
                    for f in range(NB):
                        ins = M.matmul(ps_m[c % 2][:, :], mean_w, w_in_sb[:, f, 512 * c:512 * (c + 1)],
                                       start=(f == 0), stop=(f == NB - 1))
                    ins.then_inc(s_mean, 1)
                pe.wait_ge(s_prep, 3)
                for b in range(ND):
                    input_product(0, b, 0, True)
                bc_product(0, 0, True)
                for b in range(ND):
                    dt_product(0, b, 0, True)

            def body(i, par):
                for n in range(NU):
                    if n >= SUM_LAG:
                        sum_states(i, n - SUM_LAG)
                    elif not is0(i):
                        sum_states(i - 1, NU + n - SUM_LAG)
                    if n in OUT_AT:
                        out_product(i, OUT_AT[n], par, par)
                    if n + NU in OUT_AT and not is0(i):
                        out_product(i - 1, OUT_AT[n + NU], 1 - par, 1 - par)
                    if n in IN_AT:
                        input_product(i + 1, IN_AT[n], par)
                    for b in GATE_AT.get(n, ()):
                        gate_product(i, b, par)
                    if n == BC_AT:
                        bc_product(i + 1, par)
                    if n in DT_AT:
                        dt_product(i + 1, DT_AT[n], par)

            def epilogue():
                for n in range(NU - SUM_LAG, NU):
                    sum_states(LAST, n)
                for n in sorted(OUT_AT):
                    if n >= NU:
                        out_product(LAST, OUT_AT[n], LAST % 2, LAST % 2)

            over_chunks(pe, prologue, body, None, epilogue)


def program(nc, inp, w_in, conv_w, conv_b, w_x, w_dt, b_dt, w_out, a_mat, d_vec, w_r, w_k, w_v, mu_r, mu_k, out):
    xs = nc.dram_tensor("xs_scratch", (BATCH, SEQ, DM), F32).ap()
    x2 = nc.dram_tensor("x2_scratch", (BATCH, SEQ, DM), F32).ap()
    hT_pad = nc.dram_tensor("hT_scratch", (P, NB, BATCH * ROW + TAIL), F32).ap()
    bc_dram = nc.dram_tensor("bc_scratch", (2 * DS, T), F32).ap()
    ffn_phase(nc, "f1", inp, w_r, w_k, w_v, mu_r, mu_k, xs, hT_pad)
    mixer_phase(nc, hT_pad, xs, w_in, conv_w, conv_b, w_x, w_dt, b_dt, w_out, a_mat, d_vec, bc_dram, x2)
    ffn_phase(nc, "f2", x2, w_r, w_k, w_v, mu_r, mu_k, out)


_INS = ["L0_attn_inp", "L0_attn_W_in", "L0_attn_conv_w", "L0_attn_conv_b", "L0_attn_W_x", "L0_attn_W_dt",
        "L0_attn_b_dt", "L0_attn_W_out", "L0_attn_A", "L0_attn_D", "L0_ffn_W_r", "L0_ffn_W_k", "L0_ffn_W_v",
        "L0_ffn_mu_r", "L0_ffn_mu_k"]


def kernel(**inputs):
    import numpy as np
    import concourse.bacc as bacc
    from concourse.bass_utils import run_bass_kernel_spmd

    nc = bacc.Bacc("TRN2", target_bir_lowering=False, num_devices=1)
    arrays, args = {}, []
    for name in _INS:
        a = np.ascontiguousarray(inputs[name])
        arrays[f"in_{name}"] = a
        args.append(nc.dram_tensor(f"in_{name}", a.shape, mybir.dt.from_np(a.dtype), kind="ExternalInput").ap())
    args.append(nc.dram_tensor("out_dram", (BATCH, SEQ, DM), F32, kind="ExternalOutput").ap())
    program(nc, *args)
    r = run_bass_kernel_spmd(nc, [arrays], core_ids=[0])
    return r.results[0]["out_dram"]
```

```python
from contextlib import ExitStack

import concourse.bass as bass
from concourse import mybir

F32 = mybir.dt.float32
F32R = mybir.dt.float32r
ALU = mybir.AluOpType
ACT = mybir.ActivationFunctionType

P = 128
BATCH, SEQ, DM = 4, 2048, 512
DI, DS, KC = 1024, 16, 4
EPS = 1e-5
NB = DM // P
ND = DI // P
PAD_L, PAD_R = 1, 2

FT = 512
FJ = FT // P
FC = SEQ // FT
NX = FC

T = 256
TJ = T // P
TH = T + PAD_L + PAD_R
MC = SEQ // T
SG = 4
NG = DS // SG
NU = NG * ND
NH = 4
ROW = SEQ + PAD_L + PAD_R
TAIL = T + TH


def ffn_phase(nc, name, x_in, w_r, w_k, w_v, mu_r, mu_k, out, hT_pad=None):
    mixer = hT_pad is not None
    x_v = x_in.rearrange("b (c j p) d -> (b c) p j d", c=FC, p=P)
    out_v = out.rearrange("b (c j p) d -> (b c) p j d", c=FC, p=P)

    with ExitStack() as ctx:
        def sb(n, shape, dt=F32):
            return ctx.enter_context(nc.sbuf_tensor(f"{name}_{n}", shape, dt))

        def sem(n):
            return ctx.enter_context(nc.semaphore(f"{name}_{n}"))

        ident = sb("ident", [P, P])
        w_hi = sb("w_hi", [P, 3, NB, DM], F32R)
        w_lo = sb("w_lo", [P, 3, NB, DM], F32R)
        mu = sb("mu", [P, 2, NB])
        half = sb("half", [P, FJ])
        x = sb("x", [P, NX, FJ, DM])
        stats = sb("stats", [P, FJ, 6])
        mv = sb("mv", [P, 2, FJ, 2])
        ve = sb("ve", [P, 2, FJ])
        rstd = sb("rstd", [P, 2, FJ])
        mark = sb("mark", [P, 1])
        hx = sb("hx", [P, FJ, DM])
        xhT = sb("xhT", [P, 2, NB, FT + 1])
        dsh = sb("dsh", [P, NB, FT])
        mix = sb("mix", [P, NB, FT])
        xr_hi = sb("xr_hi", [P, NB, FT], F32R)
        xr_lo = sb("xr_lo", [P, NB, FT], F32R)
        xk_hi = sb("xk_hi", [P, NB, FT], F32R)
        xk_lo = sb("xk_lo", [P, NB, FT], F32R)
        ka = sb("ka", [P, NB, FT])
        ka_hi = sb("ka_hi", [P, NB, FT], F32R)
        ka_lo = sb("ka_lo", [P, NB, FT], F32R)
        rt = sb("rt", [P, FJ, DM])
        h2 = sb("h2", [P, FJ, DM]) if mixer else None
        h2T = sb("h2T", [P, NB, TAIL]) if mixer else None
        zpad = h2T
        w_nat = (rt, ka, dsh)

        ps_kr = [ctx.enter_context(nc.psum_tensor(f"{name}_ps_kr{n}", [P, 512], F32)) for n in range(2)]
        ps_v = [ctx.enter_context(nc.psum_tensor(f"{name}_ps_v{n}", [P, 512], F32)) for n in range(2)]
        ps_t = [ctx.enter_context(nc.psum_tensor(f"{name}_ps_t{n}", [P, 512], F32)) for n in range(2)]

        s_id = sem("ident_made")
        s_w = sem("weights_loaded")
        s_x = [sem(f"x_loaded{n}") for n in range(NX)]
        s_wt = sem("weight_transposed")
        s_wh = sem("weight_high_ready")
        s_wc = sem("weight_split")
        s_st = sem("ln_chain")
        s_ve = sem("variance_ready")
        s_rs = sem("rstd_ready")
        s_hx = sem("hx_ready")
        s_t = sem("transposed")
        s_tc = sem("xhT_ready")
        s_prev = sem("prev_column_ready")
        s_dsh = sem("dsh_ready")
        s_mk = sem("xk_mixed")
        s_mr = sem("xr_mixed")
        s_hi = sem("mix_high_ready")
        s_xk = sem("xk_ready")
        s_xr = sem("xr_ready")
        s_kr = sem("kr_in_psum")
        s_kre = sem("kr_evacuated")
        s_sq = sem("relu_squared")
        s_relu = sem("ka_high_ready")
        s_ka = sem("ka_ready")
        s_v = sem("v_in_psum")
        s_vt = sem("v_used")
        s_x1 = sem("x1_ready")
        s_h2 = sem("h2_ready")
        s_xs = sem("xs_ready")
        s_t2 = sem("h2_transposed")
        s_t2c = sem("h2T_ready")
        s_pad = sem("pad_zeroed")
        s_out = sem("out_stored")
        s_ht = sem("hT_stored")
        block = ctx.enter_context(nc.Block())

        def over_chunks(eng, prologue, body):
            if prologue:
                prologue()
            with eng.Fori(0, BATCH - 1) as b:
                for c in range(FC):
                    body(b, c, FC * b + c, 0)
            for c in range(FC):
                body(BATCH - 1, c, FC * (BATCH - 1) + c, FC - c)


        def norms_before_2(i, left):
            return 2 * i + 3 - {1: 2, 2: 1}.get(left, 0)

        @block.sync
        def _(sp):
            for n, w in enumerate((w_r, w_k, w_v)):
                sp.dma_start(w_nat[n][:, :, :], w.rearrange("(o p) c -> p o c", p=P)).then_inc(s_w, 16)
            for n, m in enumerate((mu_r, mu_k)):
                sp.dma_start(mu[:, n, :], m.rearrange("(o p) -> p o", p=P),
                             allow_slow_non_contiguous=True).then_inc(s_w, 16)
            for c in range(NX):
                sp.dma_start(x[:, c], x_v[c]).then_inc(s_x[c], 16)
            if mixer:
                sp.wait_ge(s_pad, 1)
                for b in range(BATCH):
                    sp.dma_start(hT_pad[:, :, b * ROW:b * ROW + PAD_L], zpad[:, :, 0:PAD_L],
                                 allow_slow_non_contiguous=True).then_inc(s_ht, 16)
                    sp.dma_start(hT_pad[:, :, (b + 1) * ROW - PAD_R:(b + 1) * ROW], zpad[:, :, 0:PAD_R]).then_inc(s_ht, 16)
                sp.dma_start(hT_pad[:, :, BATCH * ROW:], zpad[:, :, :]).then_inc(s_ht, 16)
            pads = (2 * BATCH + 1) * 16 if mixer else 0

            def body(b, c, i, left):
                sp.wait_ge(s_xs if mixer else s_x1, i + 1)
                sp.dma_start(out_v[i], x[:, c]).then_inc(s_out, 16)
                if left == 0:
                    sp.wait_ge(s_out, 16 * (i + 1))
                    sp.dma_start(x[:, c], x_v[i + NX]).then_inc(s_x[c], 16)
                if mixer:
                    sp.wait_ge(s_t2c, NB * (i + 1))
                    sp.dma_start(hT_pad[:, :, bass.ds(ROW * b + PAD_L + c * FT, FT)], h2T[:, :, 0:FT]).then_inc(s_ht, 16)

            over_chunks(sp, None, body)
            sp.wait_ge(s_out, 16 * BATCH * FC)
            if mixer:
                sp.wait_ge(s_ht, pads + 16 * BATCH * FC)

        @block.gpsimd
        def _(pool):
            nc.gpsimd.memset(ident[:, :], 0.0).then_inc(s_id, 1)
            nc.gpsimd.memset(half[:, :], -0.5).then_inc(s_id, 1)
            pool.wait_ge(s_id, 2)
            nc.gpsimd.affine_select(out=ident[:, :], in_=ident[:, :], compare_op=ALU.not_equal, fill=1.0,
                                    base=0, pattern=[[-1, P]], channel_multiplier=1).then_inc(s_id, 1)
            if mixer:
                nc.gpsimd.memset(zpad[:, :, :], 0.0).then_inc(s_pad, 1)
            def power(which, k):
                pool.wait_ge(s_ve, k + 1)
                nc.gpsimd.tensor_tensor(rstd[:, which], ve[:, which], half[:, :], ALU.pow).then_inc(s_rs, 1)

            def shift(i, slot):
                pool.wait_ge(s_tc, NB * (i + 1))
                pool.wait_ge(s_prev, i + 1)
                if not (isinstance(i, int) and i == 0):
                    pool.wait_ge(s_xr, i)
                nc.gpsimd.tensor_tensor(dsh[:, :, :], xhT[:, slot, :, 1:FT + 1], xhT[:, slot, :, 0:FT],
                                        ALU.subtract).then_inc(s_dsh, 1)

            def prologue():
                power(0, 0)
                shift(0, 0)
                power(0, 1)
                shift(1, 1)
                power(0, 2)

            def body(b, c, i, left):
                if left == 0 or left > 2:
                    shift(i + 2, c % 2)
                if mixer:
                    power(1, norms_before_2(i, left))
                    pool.wait_ge(s_h2, FJ * (i + 1))
                    nc.gpsimd.tensor_tensor(x[:, c], x[:, c], h2[:, :, :], ALU.add).then_inc(s_xs, 1)
                if left == 0 or left > 3:
                    power(0, norms_before_2(i, left) + 1 if mixer else i + 3)

            over_chunks(pool, prologue, body)

        @block.scalar
        def _(act):
            def copy_weights():
                for g in range(3 * NB):
                    act.wait_ge(s_wt, g + 1)
                    nc.scalar.activation(w_hi[:, g // NB, g % NB, :], ps_t[g % 2][:, :], ACT.Copy).then_inc(s_wh, 1)

            def copy_xhT(i, slot, seq_start):
                if not (isinstance(i, int) and i < 2):
                    act.wait_ge(s_xr, i - 1)
                if seq_start:
                    nc.scalar.activation(xhT[:, slot, :, 0], ident[:, 0:NB], ACT.Copy, scale=0.0).then_inc(s_prev, 1)
                else:
                    act.wait_ge(s_tc, NB * i)
                    nc.scalar.activation(xhT[:, slot, :, 0], xhT[:, 1 - slot, :, FT], ACT.Copy).then_inc(s_prev, 1)
                for f in range(NB):
                    act.wait_ge(s_t, NB * i + f + 1)
                    nc.scalar.activation(xhT[:, slot, f, 1:FT + 1], ps_t[f % 2][:, :], ACT.Copy).then_inc(s_tc, 1)

            def high_xk(i):
                if not (isinstance(i, int) and i == 0):
                    act.wait_ge(s_kr, 2 * NB * i - NB)
                act.wait_ge(s_mk, NB * (i + 1))
                nc.scalar.activation(xk_hi[:, :, :], mix[:, :, :], ACT.Copy).then_inc(s_hi, 1)

            def high_xr(i):
                if not (isinstance(i, int) and i == 0):
                    act.wait_ge(s_kr, 2 * NB * i)
                act.wait_ge(s_mr, NB * (i + 1))
                nc.scalar.activation(xr_hi[:, :, :], mix[:, :, :], ACT.Copy).then_inc(s_hi, 1)

            def copy_k(i):
                for d in range(NB):
                    act.wait_ge(s_kr, 2 * NB * i + d + 1)
                    nc.scalar.activation(ka[:, d, :], ps_kr[d % 2][:, :], ACT.Relu).then_inc(s_kre, 1)
                    act.wait_ge(s_kre, 2 * NB * i + d + 1)
                    nc.scalar.activation(ka[:, d, :], ka[:, d, :], ACT.Square).then_inc(s_sq, 1)
                    act.wait_ge(s_sq, NB * i + d + 1)
                    nc.scalar.activation(ka_hi[:, d, :], ka[:, d, :], ACT.Copy).then_inc(s_relu, 1)

            def copy_r(i):
                if not (isinstance(i, int) and i == 0):
                    act.wait_ge(s_x1, i)
                for j in range(FJ):
                    act.wait_ge(s_kr, 2 * NB * i + NB + j + 1)
                    nc.scalar.activation(rt[:, j, :], ps_kr[j % 2][:, :], ACT.Tanh, scale=0.5).then_inc(s_kre, 1)

            def prologue():
                act.wait_ge(s_id, 3)
                copy_weights()
                copy_xhT(0, 0, True)
                high_xk(0)
                high_xr(0)
                copy_k(0)
                copy_xhT(1, 1, False)
                high_xk(1)
                copy_r(0)
                high_xr(1)

            def body(b, c, i, left):
                if left == 0 or left > 2:
                    copy_xhT(i + 2, c % 2, c + 2 == FC)
                if left == 0 or left > 1:
                    copy_k(i + 1)
                if mixer:
                    act.wait_ge(s_ht, (2 * BATCH + 1) * 16 + 16 * i)
                    for f in range(NB):
                        act.wait_ge(s_t2, NB * i + f + 1)
                        nc.scalar.activation(h2T[:, f, 0:FT], ps_t[f % 2][:, :], ACT.Copy).then_inc(s_t2c, 1)
                if left == 0 or left > 2:
                    high_xk(i + 2)
                if left == 0 or left > 1:
                    copy_r(i + 1)
                if left == 0 or left > 2:
                    high_xr(i + 2)

            over_chunks(act, prologue, body)

        @block.vector
        def _(dve):
            V = nc.vector
            def norm(which, src, dst, k, done, before):
                st = 2 * FJ * k
                for j in range(FJ):
                    V.bn_stats(out=stats[:, j, :], in_=src[:, j, :]).then_inc(s_st, 1)
                dve.wait_ge(s_st, st + FJ)
                V.memset(mark[:, :], 0.0)
                for j in range(FJ):
                    V.bn_aggr(out=mv[:, which, j, :], in_=stats[:, j, :]).then_inc(s_st, 1)
                dve.wait_ge(s_st, st + 2 * FJ)
                V.tensor_scalar(ve[:, which], mv[:, which, :, 1], EPS, None, ALU.add).then_inc(s_ve, 1)
                dve.wait_ge(s_rs, k + 1)
                before()
                for j in range(FJ):
                    V.tensor_scalar(dst[:, j, :], src[:, j, :], mv[:, which, j, 0:1], rstd[:, which, j:j + 1],
                                    ALU.subtract, ALU.mult).then_inc(done, 1)

            def norm1(i, slot, k, nth):
                dve.wait_ge(s_x[slot], 16 * nth)

                def free():
                    if not (isinstance(i, int) and i == 0):
                        dve.wait_ge(s_t, NB * i)
                norm(0, x[:, slot], hx, k, s_hx, free)

            def mixed(i, slot, n, lo, hi, done, low):
                dve.wait_ge(s_dsh, i + 1)
                if n == 0:
                    dve.wait_ge(s_xk, i + 1)
                elif not (isinstance(i, int) and i == 0):
                    dve.wait_ge(s_xr, i)
                for f in range(NB):
                    V.scalar_tensor_tensor(out=mix[:, f, :], in0=dsh[:, f, :], scalar=mu[:, n, f:f + 1],
                                           in1=xhT[:, slot, f, 0:FT], op0=ALU.mult, op1=ALU.add).then_inc(done, 1)
                dve.wait_ge(s_hi, 2 * i + 2 - n)
                V.tensor_tensor(lo[:, :, :], mix[:, :, :], hi[:, :, :].bitcast(F32), ALU.subtract).then_inc(low, 1)

            def mixed_k(i, slot):
                mixed(i, slot, 1, xk_lo, xk_hi, s_mk, s_xk)

            def mixed_r(i, slot):
                mixed(i, slot, 0, xr_lo, xr_hi, s_mr, s_xr)

            def split_k(i):
                for d in range(NB):
                    dve.wait_ge(s_relu, NB * i + d + 1)
                    V.tensor_tensor(ka_lo[:, d, :], ka[:, d, :], ka_hi[:, d, :].bitcast(F32),
                                    ALU.subtract).then_inc(s_ka, 1)

            dve.wait_ge(s_w, 5 * 16)
            for g in range(3 * NB):
                dve.wait_ge(s_wh, g + 1)
                V.tensor_tensor(w_lo[:, g // NB, g % NB, :], ps_t[g % 2][:, :],
                                w_hi[:, g // NB, g % NB, :].bitcast(F32), ALU.subtract).then_inc(s_wc, 1)
            norm1(0, 0, 0, 1)
            mixed_k(0, 0)
            mixed_r(0, 0)
            norm1(1, 1, 1, 1)
            split_k(0)
            mixed_k(1, 1)
            norm1(2, 2, 2, 1)
            mixed_r(1, 1)

            def body(b, c, i, left):
                for j in range(FJ):
                    dve.wait_ge(s_v, FJ * i + j + 1)
                    dve.wait_ge(s_kre, 2 * NB * i + NB + j + 1)
                    V.scalar_tensor_tensor(out=rt[:, j, :], in0=rt[:, j, :], scalar=1.0, in1=ps_v[j % 2][:, :],
                                           op0=ALU.add, op1=ALU.mult).then_inc(s_vt, 1)
                dve.wait_ge(s_vt, FJ * (i + 1))
                for j in range(FJ):
                    ins = V.scalar_tensor_tensor(out=x[:, c, j, :], in0=rt[:, j, :], scalar=0.25,
                                                 in1=x[:, c, j, :], op0=ALU.mult, op1=ALU.add)
                ins.then_inc(s_x1, 1)
                if mixer:
                    dve.wait_ge(s_x1, i + 1)

                    def free():
                        if left in (1, 2):
                            dve.wait_ge(s_t2, NB * i)
                            dve.wait_ge(s_xs, i)
                    norm(1, x[:, c], h2, norms_before_2(i, left), s_h2, free)
                if left == 0 or left > 1:
                    split_k(i + 1)
                if left == 0 or left > 2:
                    mixed_k(i + 2, c % 2)
                if left == 0 or left > 3:
                    nth = (b if c + 3 < FC else b + 1) + 1
                    norm1(i + 3, (c + 3) % NX, norms_before_2(i, left) + 1 if mixer else i + 3, nth)
                if left == 0 or left > 2:
                    mixed_r(i + 2, c % 2)

            over_chunks(dve, None, body)

        @block.tensor
        def _(pe):
            M = nc.tensor

            def turn_weights():
                for g in range(3 * NB):
                    if g >= 2:
                        pe.wait_ge(s_wc, g - 1)
                    for o in range(NB):
                        ins = M.transpose(ps_t[g % 2][:, o * P:(o + 1) * P],
                                          w_nat[g // NB][:, o, (g % NB) * P:(g % NB + 1) * P], ident[:, :])
                    ins.then_inc(s_wt, 1)

            def turn(i, src, ready, done, copied_before):
                pe.wait_ge(ready, FJ * (i + 1))
                for f in range(NB):
                    copied_before(f)
                    for j in range(FJ):
                        ins = M.transpose(ps_t[f % 2][:, j * P:(j + 1) * P], src[:, j, f * P:(f + 1) * P], ident[:, :])
                    ins.then_inc(done, 1)

            def turn1(i):
                def bank(f):
                    if f >= 2:
                        pe.wait_ge(s_tc, NB * i + f - 1)
                    elif mixer and not (isinstance(i, int) and i < 3):
                        pe.wait_ge(s_t2c, NB * (i - 2))
                    elif isinstance(i, int) and i == 0:
                        pe.wait_ge(s_wc, 3 * NB)
                    else:
                        pe.wait_ge(s_tc, NB * i)
                turn(i, hx, s_hx, s_t, bank)

            def turn2(i):
                def bank(f):
                    if f >= 2:
                        pe.wait_ge(s_t2c, NB * i + f - 1)
                    elif isinstance(i, int) and i >= BATCH * FC - 2:
                        pe.wait_ge(s_tc, NB * BATCH * FC)
                        if i == BATCH * FC - 1:
                            pe.wait_ge(s_t2c, NB * i)
                    else:
                        pe.wait_ge(s_tc, NB * (i + 3))
                turn(i, h2, s_h2, s_t2, bank)

            def bank_free(n, first):
                if not (first and n < 2):
                    pe.wait_ge(s_kre, n - 1)

            def split_product(ps, terms):
                last = len(terms) - 1
                for n, (a_hi, a_lo, b_hi, b_lo) in enumerate(terms):
                    M.matmul(ps, a_hi, b_lo, start=(n == 0), stop=False)
                    M.matmul(ps, a_hi, b_hi, start=False, stop=False)
                    ins = M.matmul(ps, a_lo, b_hi, start=False, stop=(n == last))
                return ins

            def k_products(i):
                pe.wait_ge(s_xk, i + 1)
                for d in range(NB):
                    bank_free(2 * NB * i + d, isinstance(i, int) and i == 0 and d < 2)
                    o = slice(d * P, (d + 1) * P)
                    ins = split_product(ps_kr[d % 2][:, :], [
                        (w_hi[:, 1, f, o], w_lo[:, 1, f, o], xk_hi[:, f, :], xk_lo[:, f, :]) for f in range(NB)])
                    ins.then_inc(s_kr, 1)

            def r_products(i):
                pe.wait_ge(s_xr, i + 1)
                for j in range(FJ):
                    bank_free(2 * NB * i + NB + j, False)
                    t = slice(j * P, (j + 1) * P)
                    ins = split_product(ps_kr[j % 2][:, :], [
                        (xr_hi[:, f, t], xr_lo[:, f, t], w_hi[:, 0, f, :], w_lo[:, 0, f, :]) for f in range(NB)])
                    ins.then_inc(s_kr, 1)

            def v_products(i, c):
                pe.wait_ge(s_ka, NB * (i + 1))
                for j in range(FJ):
                    if j >= 2 or not (c == 0):
                        pe.wait_ge(s_vt, FJ * i + (j - 1 if j >= 2 else 0))
                    t = slice(j * P, (j + 1) * P)
                    ins = split_product(ps_v[j % 2][:, :], [
                        (ka_hi[:, d, t], ka_lo[:, d, t], w_hi[:, 2, d, :], w_lo[:, 2, d, :]) for d in range(NB)])
                    ins.then_inc(s_v, 1)

            def prologue():
                pe.wait_ge(s_id, 3)
                pe.wait_ge(s_w, 5 * 16)
                turn_weights()
                turn1(0)
                k_products(0)
                turn1(1)
                r_products(0)

            def body(b, c, i, left):
                if left == 0 or left > 2:
                    turn1(i + 2)
                v_products(i, c)
                if left == 0 or left > 1:
                    k_products(i + 1)
                if mixer:
                    turn2(i)
                if left == 0 or left > 1:
                    r_products(i + 1)

            over_chunks(pe, prologue, body)


def bcast(ap, n):
    return ap.unsqueeze(1).to_broadcast([ap.shape[0], n, ap.shape[1]])


def mixer_phase(nc, hT_pad, xs_in, w_in, conv_w, conv_b, w_x, w_dt, b_dt, w_out, a_mat, d_vec, bc_dram, out):
    xs_v = xs_in.rearrange("b (c j p) d -> (b c) p j d", c=MC, p=P)
    out_v = out.rearrange("b (c j p) d -> (b c) p j d", c=MC, p=P)
    LAST = BATCH * MC - 1

    with ExitStack() as ctx:
        def sb(n, shape):
            return ctx.enter_context(nc.sbuf_tensor(f"mx_{n}", shape, F32))

        def sem(n):
            return ctx.enter_context(nc.semaphore(f"mx_{n}"))

        ident = sb("ident", [P, P])
        w_in_sb = sb("w_in", [P, NB, 2 * DI])
        w_x_sb = sb("w_x", [P, ND, 2 * DS])
        w_dt_sb = sb("w_dt", [P, ND, DI])
        w_out_sb = sb("w_out", [P, ND, DM])
        cw = sb("cw", [P, KC, ND])
        cb = sb("cb", [P, ND])
        bdt = sb("bdt", [P, ND])
        a_sb = sb("a", [P, ND, DS])
        d_sb = sb("d", [P, ND])
        hst = sb("hst", [P, ND, DS])
        hT = sb("hT", [P, 2, NB, TH])
        u = sb("u", [P, 2, ND, T])
        dl = sb("dl", [P, 2, ND, T])
        du = sb("du", [P, ND, T])
        ex = sb("ex", [P, ND, T])
        zs = sb("zs", [P, ND, T])
        bs = sb("bs", [P, NG, SG, T])
        cs = sb("cs", [P, NG, SG, T])
        bc = sb("bc", [2 * DS, T])
        dbu = sb("dbu", [P, 2, SG, T])
        hp = sb("hp", [P, NH, SG, T])
        xo = sb("xo", [P, TJ, DM])

        ps_y = ctx.enter_context(nc.psum_tensor("mx_ps_y", [P, ND, T], F32))
        ps_da = [ctx.enter_context(nc.psum_tensor(f"mx_ps_da{n}", [P, 2, T], F32)) for n in range(2)]
        ps_m = [ctx.enter_context(nc.psum_tensor(f"mx_ps_m{n}", [P, 512], F32)) for n in range(2)]

        s_id = sem("ident_made")
        s_w = sem("weights_loaded")
        s_mean = sem("w_in_mean")
        s_cen = sem("w_in_centred")
        s_prep = sem("weights_scaled")
        s_ht = [sem(f"hT_loaded{n}") for n in range(2)]
        s_pi = sem("input_in_psum")
        s_pz = sem("gate_in_psum")
        s_pb = sem("bc_in_psum")
        s_pd = sem("dt_in_psum")
        s_po = sem("out_in_psum")
        s_cv = sem("conv_steps")
        s_cq = sem("conv_ready")
        s_ct = sem("conv_tanh")
        s_u = sem("u_ready")
        s_bc = sem("bc_copied")
        s_bcd = sem("bc_stored")
        s_bl = [sem(f"b_loaded{n}") for n in range(NG)]
        s_cl = [sem(f"c_loaded{n}") for n in range(NG)]
        s_c0 = sem("conv_tap0")
        s_ab = sem("dt_abs")
        s_sp = sem("softplus_steps")
        s_dl = sem("delta_ready")
        s_du = sem("du_ready")
        s_m1 = sem("dbu_ready")
        s_da = sem("da_ready")
        s_sc = sem("scanned")
        s_m2 = sem("hc_ready")
        s_pr = sem("pairs_added")
        s_r = sem("states_summed")
        s_st = sem("state_kept")
        s_zt = sem("z_tanh")
        s_zs = sem("zs_ready")
        s_yd = sem("yd_ready")
        s_g = sem("gated")
        s_x = sem("xs_loaded")
        s_o = sem("out_ready")
        s_out = sem("out_stored")
        s_rst = sem("state_zeroed")
        block = ctx.enter_context(nc.Block())

        mean_w = hp[:, 0, 0, 0:P]

        IN_AT = {n: b for b, n in enumerate((6, 7, 8, 10, 11, 12, 14, 15))}
        GATE_AT = {9: (0, 1), 13: (2, 3), 16: (4, 5), 17: (6, 7)}
        BC_AT = 18
        DT_AT = {19 + b: b for b in range(ND)}
        OUT_AT = {31: (0, 1), NU: (2, 3), NU + 2: (4, 5), NU + 4: (6, 7)}
        YG_AT = {29: 0, 31: 1, NU + 1: 2, NU + 3: 3}
        EVAC_AT = 5
        LN_AT, ADD_AT = 28, 30
        PAIR_LAG, SUM_LAG = 2, 3
        PAIR = ND
        order = []
        for n in range(NU):
            if n in IN_AT:
                order.append(("in", IN_AT[n]))
            order += [("gate", b) for b in GATE_AT.get(n, ())]
            if n == BC_AT:
                order.append(("bc", 0))
            if n in DT_AT:
                order.append(("dt", DT_AT[n]))
        order += [("out", 0), ("out", 1)]
        first_order = [("in", b) for b in range(ND)] + [("bc", 0)] + [("dt", b) for b in range(ND)]

        def bank(kind, b, i, par, first=False):
            if first:
                return ps_m[first_order.index((kind, b)) % 2]
            return ps_m[(len(first_order) + len(order) * par + order.index((kind, b))) % 2]

        def over_chunks(eng, prologue, body, sequence=None, epilogue=None):
            if prologue:
                prologue()
            if sequence:
                sequence(0)
            body(0, 0)
            body(1, 1)
            with eng.Fori(1, MC // 2) as c2:
                for par in range(2):
                    body(2 * c2 + par, par)
            with eng.Fori(1, BATCH) as b:
                if sequence:
                    sequence(b)
                with eng.Fori(0, MC // 2) as c2:
                    for par in range(2):
                        body(MC * b + 2 * c2 + par, par)
            if epilogue:
                epilogue()

        def is0(i):
            return isinstance(i, int) and i == 0

        @block.sync
        def _(sp):
            for dst, src in (
                (w_in_sb[:, :, :], w_in.rearrange("(f p) n -> p f n", p=P)),
                (w_dt_sb[:, :, :], w_dt.rearrange("(f p) n -> p f n", p=P)),
                (w_out_sb[:, :, :], w_out.rearrange("(f p) n -> p f n", p=P)),
                (w_x_sb[:, :, :], w_x.rearrange("(f p) n -> p f n", p=P)),
                (a_sb[:, :, :], a_mat.rearrange("(f p) n -> p f n", p=P)),
                (cw[:, :, :], conv_w.rearrange("k o (f p) -> p (k o) f", p=P)),
                (cb[:, :], conv_b.rearrange("(f p) -> p f", p=P)),
                (bdt[:, :], b_dt.rearrange("(f p) -> p f", p=P)),
                (d_sb[:, :], d_vec.rearrange("(f p) -> p f", p=P)),
            ):
                sp.dma_start(dst, src, allow_slow_non_contiguous=True).then_inc(s_w, 16)

            def load_hT(b, c, par):
                sp.dma_start(hT[:, par], hT_pad[:, :, bass.ds(ROW * b + T * c, TH)]).then_inc(s_ht[par], 16)

            def load_bc(i, units, between=None):
                sp.wait_ge(s_bc, i + 1)
                if units is not None:
                    for g in range(NG):
                        sp.wait_ge(s_bl[g], 16 * i)
                        sp.wait_ge(s_cl[g], 16 * i)
                sp.dma_start(bc_dram[:, :], bc[:, :]).then_inc(s_bcd, 16)
                sp.wait_ge(s_bcd, 16 * (i + 1))
                for g in range(NG):
                    for dst, done, first, used in ((bs, s_bl, 0, s_m1), (cs, s_cl, DS, s_m2)):
                        if units is not None:
                            sp.wait_ge(used, units + ND * (g + 1))
                        rows = bc_dram[first + SG * g:first + SG * (g + 1), :].rearrange("s t -> (s t)")
                        sp.dma_start(dst[:, g].rearrange("p s t -> p (s t)"),
                                     rows.unsqueeze(0).to_broadcast([P, SG * T])).then_inc(done[g], 16)
                    if g == NG - 2 and between:
                        between()

            def chunk(i, par, b_next, c_next):
                if not is0(i):
                    sp.wait_ge(s_out, 16 * i)
                sp.dma_start(xo[:, :, :], xs_v[i]).then_inc(s_x, 16)

                def columns():
                    sp.wait_ge(s_zs, ND * (i + 1))
                    load_hT(b_next, c_next, par)
                load_bc(i + 1, NU * i, columns)
                sp.wait_ge(s_o, i + 1)
                sp.dma_start(out_v[i], xo[:, :, :]).then_inc(s_out, 16)

            load_hT(0, 0, 0)
            load_hT(0, 1, 1)
            load_bc(0, None)
            def last_pair(b):
                for par in range(2):
                    chunk(MC * b + MC - 2 + par, par, b + 1, par)

            for par in range(2):
                chunk(par, par, 0, 2 + par)
            with sp.Fori(1, MC // 2 - 1) as c2:
                for par in range(2):
                    chunk(2 * c2 + par, par, 0, 2 * c2 + 2 + par)
            last_pair(0)
            with sp.Fori(1, BATCH) as b:
                with sp.Fori(0, MC // 2 - 1) as c2:
                    for par in range(2):
                        chunk(MC * b + 2 * c2 + par, par, b, 2 * c2 + 2 + par)
                last_pair(b)
            sp.wait_ge(s_out, 16 * (LAST + 1))

        @block.gpsimd
        def _(pool):
            G = nc.gpsimd
            G.memset(ident[:, :], 0.0).then_inc(s_id, 1)
            G.memset(mean_w, 1.0 / DM).then_inc(s_id, 1)
            pool.wait_ge(s_id, 2)
            G.affine_select(out=ident[:, :], in_=ident[:, :], compare_op=ALU.not_equal, fill=1.0,
                            base=0, pattern=[[-1, P]], channel_multiplier=1).then_inc(s_id, 1)

            def pairs(i, n):
                k = n % NH
                pool.wait_ge(s_m2, NU * i + n + 1)
                G.tensor_tensor(hp[:, k, 0:2, :], hp[:, k, 0:2, :], hp[:, k, 2:4, :], ALU.add).then_inc(s_pr, 1)

            def body(i, par):
                for n in range(NU):
                    g, b = divmod(n, ND)
                    if n == 0:
                        pool.wait_ge(s_dl, i + 1)
                    if g == 0:
                        G.tensor_tensor(du[:, b, :], dl[:, par, b, :], u[:, par, b, :], ALU.mult).then_inc(s_du, 1)
                    if b == 0:
                        pool.wait_ge(s_bl[g], 16 * (i + 1))
                    if g == 0:
                        pool.wait_ge(s_du, ND * i + b + 1)
                    if not (is0(i) and n < 2):
                        pool.wait_ge(s_sc, 2 * NU * i + 2 * (n - 1))
                    G.tensor_tensor(dbu[:, n % 2], bs[:, g], bcast(du[:, b, :], SG), ALU.mult).then_inc(s_m1, 1)
                    if n - PAIR_LAG >= PAIR:
                        pairs(i, n - PAIR_LAG)
                    elif n < PAIR_LAG and not is0(i):
                        pairs(i - 1, NU + n - PAIR_LAG)

            over_chunks(pool, None, body, None, lambda: [pairs(LAST, n) for n in range(NU - PAIR_LAG, NU)])

        @block.scalar
        def _(act):
            A = nc.scalar

            def conv_tanh(i, b):
                act.wait_ge(s_cq, ND * i + b + 1)
                A.activation(ex[:, b, :], u_of(i)[:, b, :], ACT.Tanh).then_inc(s_ct, 1)

            slots = {}

            def u_of(i):
                return u[:, slots["next"]]

            def copy_bc(i, par, first=False):
                act.wait_ge(s_pb, i + 1)
                if not is0(i):
                    act.wait_ge(s_bcd, 16 * i)
                A.activation(bc[:, :], bank("bc", 0, i, par, first)[0:2 * DS, 0:T], ACT.Copy).then_inc(s_bc, 1)

            def tap0(i, b, ps):
                act.wait_ge(s_pi, ND * i + b + 1)
                act.wait_ge(s_prep, 3)
                A.activation(u_of(i)[:, b, :], ps[:, 0:T], ACT.Identity, scale=cw[:, 0, b:b + 1],
                             bias=cb[:, b:b + 1]).then_inc(s_c0, 1)

            def exp_neg(i, b, slot, ps):
                act.wait_ge(s_pd, ND * i + b + 1)
                A.activation(dl[:, slot, b, :], ps[:, 0:T], ACT.Relu, bias=bdt[:, b:b + 1])
                A.activation(ex[:, b, :], ps[:, 0:T], ACT.Abs, bias=bdt[:, b:b + 1]).then_inc(s_ab, 1)
                act.wait_ge(s_ab, ND * i + b + 1)
                A.activation(ex[:, b, :], ex[:, b, :], ACT.Exp, scale=-1.0).then_inc(s_sp, 1)

            def log(i):
                act.wait_ge(s_sp, (ND + 1) * i + ND)
                A.activation(ex[:, :, :], ex[:, :, :], ACT.Ln, bias=1.0).then_inc(s_sp, 1)

            def gate_tanh(i, par, b):
                act.wait_ge(s_pz, ND * i + b + 1)
                A.activation(zs[:, b, :], bank("gate", b, i, par)[:, 0:T], ACT.Tanh, scale=0.5).then_inc(s_zt, 1)

            def prologue():
                slots["next"] = 0
                for b in range(ND):
                    tap0(0, b, bank("in", b, 0, 0, True))
                    conv_tanh(0, b)
                copy_bc(0, 0, True)
                for b in range(ND):
                    exp_neg(0, b, 0, bank("dt", b, 0, 0, True))
                log(0)

            def body(i, par):
                slots["next"] = 1 - par
                for n in range(NU):
                    g, b = divmod(n, ND)
                    if n == 0:
                        act.wait_ge(s_dl, i + 1)
                    for half in range(2):
                        if not (is0(i) and n == 0):
                            act.wait_ge(s_sc, 2 * NU * i + 2 * n - 1 + half + (1 if n == 0 and half == 0 else 0))
                        for k in range(2):
                            s = SG * g + 2 * half + k
                            ins = A.activation(ps_da[half][:, k, :], dl[:, par, b, :], ACT.Exp, scale=a_sb[:, b, s:s + 1])
                        ins.then_inc(s_da, 1)
                        if half == 0 and n - 1 in IN_AT:
                            tap0(i + 1, IN_AT[n - 1], bank("in", IN_AT[n - 1], i, par))
                    if n - 2 in IN_AT:
                        conv_tanh(i + 1, IN_AT[n - 2])
                    if n - 1 == BC_AT:
                        copy_bc(i + 1, par)
                    for bb in GATE_AT.get(n - 1, ()):
                        gate_tanh(i, par, bb)
                    if n - 2 in DT_AT:
                        exp_neg(i + 1, DT_AT[n - 2], 1 - par, bank("dt", DT_AT[n - 2], i, par))
                    if n == LN_AT:
                        log(i + 1)

            act.wait_ge(s_w, 16 * 9)
            over_chunks(act, prologue, body)

        @block.vector
        def _(dve):
            V = nc.vector

            def weights():
                dve.wait_ge(s_w, 16 * 9)
                V.tensor_scalar(cw[:, :, :], cw[:, :, :], 0.5, None, ALU.mult).then_inc(s_prep, 1)
                V.tensor_scalar(cb[:, :], cb[:, :], 0.5, None, ALU.mult).then_inc(s_prep, 1)
                V.tensor_scalar(w_out_sb[:, :, :], w_out_sb[:, :, :], 0.5, None, ALU.mult).then_inc(s_prep, 1)
                for c in range(2 * DI // 512):
                    dve.wait_ge(s_mean, c + 1)
                    for f in range(NB):
                        w = w_in_sb[:, f, 512 * c:512 * (c + 1)]
                        ins = V.tensor_tensor(w, w, ps_m[c % 2][:, :], ALU.subtract)
                    ins.then_inc(s_cen, 1)
                dve.wait_ge(s_prep, 3)

            def conv(i, b, step, slot, ps):
                q = u[:, slot, b, :]
                if step == 1:
                    dve.wait_ge(s_c0, ND * i + b + 1)
                else:
                    dve.wait_ge(s_cv, (KC - 2) * (ND * i + b) + step - 1)
                V.scalar_tensor_tensor(out=q, in0=ps[:, step:step + T], scalar=cw[:, step, b:b + 1], in1=q,
                                       op0=ALU.mult, op1=ALU.add).then_inc(s_cq if step == KC - 1 else s_cv, 1)

            def silu(i, b, slot):
                dve.wait_ge(s_ct, ND * i + b + 1)
                q = u[:, slot, b, :]
                V.scalar_tensor_tensor(out=q, in0=ex[:, b, :], scalar=1.0, in1=q, op0=ALU.add, op1=ALU.mult).then_inc(s_u, 1)

            def add_log(i, slot):
                dve.wait_ge(s_sp, (ND + 1) * (i + 1))
                V.tensor_tensor(dl[:, slot], dl[:, slot], ex[:, :, :], ALU.add).then_inc(s_dl, 1)

            def gate(i, b, ps):
                dve.wait_ge(s_zt, ND * i + b + 1)
                V.scalar_tensor_tensor(out=zs[:, b, :], in0=zs[:, b, :], scalar=1.0, in1=ps[:, 0:T],
                                       op0=ALU.add, op1=ALU.mult).then_inc(s_zs, 1)

            def gated(i, j, slot):
                dve.wait_ge(s_r, NU * i + NU - ND + 2 * j + 2)
                for b in (2 * j, 2 * j + 1):
                    V.scalar_tensor_tensor(out=u[:, slot, b, :], in0=u[:, slot, b, :], scalar=d_sb[:, b:b + 1],
                                           in1=ps_y[:, b, :], op0=ALU.mult, op1=ALU.add).then_inc(s_yd, 1)
                dve.wait_ge(s_yd, ND * i + 2 * j + 2)
                dve.wait_ge(s_zs, ND * (i + 1))
                for b in (2 * j, 2 * j + 1):
                    V.tensor_tensor(u[:, slot, b, :], u[:, slot, b, :], zs[:, b, :], ALU.mult).then_inc(s_g, 1)

            def residual(i, par):
                dve.wait_ge(s_po, i + 1)
                dve.wait_ge(s_x, 16 * (i + 1))
                for j in range(TJ):
                    ins = V.tensor_tensor(xo[:, j, :], bank("out", j, i, par)[:, :], xo[:, j, :], ALU.add)
                ins.then_inc(s_o, 1)

            def keep(i, n):
                g, b = divmod(n, ND)
                dve.wait_ge(s_sc, 2 * (NU * i + n + 1))
                V.tensor_copy(hst[:, b, SG * g:SG * (g + 1)], hp[:, n % NH, :, T - 1]).then_inc(s_st, 1)

            def times_c(i, n):
                g, b = divmod(n, ND)
                if b == 0:
                    dve.wait_ge(s_cl[g], 16 * (i + 1))
                h = hp[:, n % NH]
                dve.wait_ge(s_st, NU * i + n + 1)
                V.tensor_tensor(h, h, cs[:, g], ALU.mult).then_inc(s_m2, 1)

            def scans(i, n, half):
                g, b = divmod(n, ND)
                dve.wait_ge(s_da, 2 * (NU * i + n) + half + 1)
                for k in range(2):
                    s = 2 * half + k
                    ins = V.tensor_tensor_scan(hp[:, n % NH, s, :], ps_da[half][:, k, :], dbu[:, n % 2, s, :],
                                               hst[:, b, SG * g + s:SG * g + s + 1], ALU.mult, ALU.add)
                ins.then_inc(s_sc, 1)

            def prologue():
                weights()
                for b in range(ND):
                    for step in range(1, KC):
                        conv(0, b, step, 0, bank("in", b, 0, 0, True))
                    silu(0, b, 0)
                add_log(0, 0)

            seq = {}

            def sequence(b):
                if not is0(b):
                    dve.wait_ge(s_st, NU * MC * b)
                V.memset(hst[:, :, :], 0.0).then_inc(s_rst, 1)
                seq["now"] = b

            def body(i, par):
                nxt = 1 - par
                for n in range(NU):
                    g, b = divmod(n, ND)
                    steps = [lambda s=s: conv(i + 1, IN_AT[n - 1], s, nxt, bank("in", IN_AT[n - 1], i, par))
                             for s in range(1, KC)] if n - 1 in IN_AT else [lambda: None] * (KC - 1)
                    if n == ADD_AT:
                        add_log(i + 1, nxt)
                    if n == 0:
                        if not is0(i):
                            dve.wait_ge(s_st, NU * i)
                        dve.wait_ge(s_rst, seq["now"] + 1)
                    dve.wait_ge(s_m1, NU * i + n + 1)
                    if not (is0(i) and n < NH):
                        dve.wait_ge(s_r, NU * i + n - NH + 1)
                    scans(i, n, 0)
                    if n > 0:
                        keep(i, n - 1)
                    steps[0]()
                    scans(i, n, 1)
                    steps[1]()
                    if n > 0:
                        times_c(i, n - 1)
                    elif not is0(i):
                        times_c(i - 1, NU - 1)
                    steps[2]()
                    if n - 2 in IN_AT:
                        silu(i + 1, IN_AT[n - 2], nxt)
                    for bb in GATE_AT.get(n - 1, ()):
                        gate(i, bb, bank("gate", bb, i, par))
                    if n in YG_AT:
                        gated(i, YG_AT[n], par)
                    if n + NU in YG_AT and not is0(i):
                        gated(i - 1, YG_AT[n + NU], nxt)
                    if n == EVAC_AT and not is0(i):
                        residual(i - 1, nxt)
                keep(i, NU - 1)

            def epilogue():
                times_c(LAST, NU - 1)
                for n in sorted(YG_AT):
                    if n >= NU:
                        gated(LAST, YG_AT[n], LAST % 2)
                residual(LAST, LAST % 2)

            over_chunks(dve, prologue, body, sequence, epilogue)

        @block.tensor
        def _(pe):
            M = nc.tensor

            def evacuated(kind, b, i):
                if kind == "in":
                    pe.wait_ge(s_cq, ND * (i + 1) + b + 1)
                elif kind == "bc":
                    pe.wait_ge(s_bc, i + 2)
                elif kind == "dt":
                    pe.wait_ge(s_ab, ND * (i + 1) + b + 1)
                elif kind == "gate":
                    pe.wait_ge(s_zs, ND * i + b + 1)
                else:
                    pe.wait_ge(s_o, i + 1)

            def bank_free(kind, b, i, first):
                if first:
                    at = first_order.index((kind, b))
                    if at >= 2:
                        evacuated(*first_order[at - 2], -1)
                    else:
                        pe.wait_ge(s_cen, 2 * DI // 512)
                    return
                at = order.index((kind, b))
                if at >= 2:
                    evacuated(*order[at - 2], i)
                elif is0(i):
                    evacuated(*first_order[at - 2], -1)
                else:
                    evacuated(*order[at - 2], i - 1)

            def input_product(i, b, par, first=False):
                bank_free("in", b, i - 1, first)
                if b == 0:
                    pe.wait_ge(s_ht[i_par(i, par, first)], 16 if first else 8 * (i - (1 - par)) + 16)
                ps = bank("in", b, i - 1, par, first)
                for f in range(NB):
                    ins = M.matmul(ps[:, 0:TH], w_in_sb[:, f, b * P:(b + 1) * P], hT[:, i_par(i, par, first), f, :],
                                   start=(f == 0), stop=(f == NB - 1))
                ins.then_inc(s_pi, 1)

            def i_par(i, par, first):
                return 0 if first else 1 - par

            def gate_product(i, b, par):
                bank_free("gate", b, i, False)
                ps = bank("gate", b, i, par)
                for f in range(NB):
                    ins = M.matmul(ps[:, 0:T], w_in_sb[:, f, DI + b * P:DI + (b + 1) * P], hT[:, par, f, PAD_L:PAD_L + T],
                                   start=(f == 0), stop=(f == NB - 1))
                ins.then_inc(s_pz, 1)

            def bc_product(i, par, first=False):
                slot = 0 if first else 1 - par
                bank_free("bc", 0, i - 1, first)
                pe.wait_ge(s_u, ND * (i + 1))
                for k in range(ND):
                    ins = M.matmul(bank("bc", 0, i - 1, par, first)[0:2 * DS, 0:T], w_x_sb[:, k, :], u[:, slot, k, :],
                                   start=(k == 0), stop=(k == ND - 1))
                ins.then_inc(s_pb, 1)

            def dt_product(i, b, par, first=False):
                slot = 0 if first else 1 - par
                bank_free("dt", b, i - 1, first)
                for k in range(ND):
                    ins = M.matmul(bank("dt", b, i - 1, par, first)[:, 0:T], w_dt_sb[:, k, b * P:(b + 1) * P],
                                   u[:, slot, k, :], start=(k == 0), stop=(k == ND - 1))
                ins.then_inc(s_pd, 1)

            def out_product(i, blocks, slot, par):
                for b in blocks:
                    pe.wait_ge(s_g, ND * i + b + 1)
                    for j in range(TJ):
                        if b == 0:
                            bank_free("out", j, i, False)
                        ins = M.matmul(bank("out", j, i, par)[:, :], u[:, slot, b, j * P:(j + 1) * P], w_out_sb[:, b, :],
                                       start=(b == 0), stop=(b == ND - 1))
                if blocks[-1] == ND - 1:
                    ins.then_inc(s_po, 1)

            def sum_states(i, n):
                g, b = divmod(n, ND)
                states = SG if n < PAIR else SG // 2
                if n < PAIR:
                    pe.wait_ge(s_m2, NU * i + n + 1)
                else:
                    pe.wait_ge(s_pr, (NU - PAIR) * i + n - PAIR + 1)
                for k in range(states):
                    ins = M.matmul(ps_y[:, b, :], ident[:, :], hp[:, n % NH, k, :],
                                   start=(g == 0 and b % 2 == 0 and k == 0), stop=(g == NG - 1 and k == states - 1),
                                   skip_group_check=True)
                ins.then_inc(s_r, 1)

            def prologue():
                pe.wait_ge(s_id, 3)
                pe.wait_ge(s_w, 16 * 9)
                for c in range(2 * DI // 512):
                    if c >= 2:
                        pe.wait_ge(s_cen, c - 1)
                    for f in range(NB):
                        ins = M.matmul(ps_m[c % 2][:, :], mean_w, w_in_sb[:, f, 512 * c:512 * (c + 1)],
                                       start=(f == 0), stop=(f == NB - 1))
                    ins.then_inc(s_mean, 1)
                pe.wait_ge(s_prep, 3)
                for b in range(ND):
                    input_product(0, b, 0, True)
                bc_product(0, 0, True)
                for b in range(ND):
                    dt_product(0, b, 0, True)

            def body(i, par):
                for n in range(NU):
                    if n >= SUM_LAG:
                        sum_states(i, n - SUM_LAG)
                    elif not is0(i):
                        sum_states(i - 1, NU + n - SUM_LAG)
                    if n in OUT_AT:
                        out_product(i, OUT_AT[n], par, par)
                    if n + NU in OUT_AT and not is0(i):
                        out_product(i - 1, OUT_AT[n + NU], 1 - par, 1 - par)
                    if n in IN_AT:
                        input_product(i + 1, IN_AT[n], par)
                    for b in GATE_AT.get(n, ()):
                        gate_product(i, b, par)
                    if n == BC_AT:
                        bc_product(i + 1, par)
                    if n in DT_AT:
                        dt_product(i + 1, DT_AT[n], par)

            def epilogue():
                for n in range(NU - SUM_LAG, NU):
                    sum_states(LAST, n)
                for n in sorted(OUT_AT):
                    if n >= NU:
                        out_product(LAST, OUT_AT[n], LAST % 2, LAST % 2)

            over_chunks(pe, prologue, body, None, epilogue)


def program(nc, inp, w_in, conv_w, conv_b, w_x, w_dt, b_dt, w_out, a_mat, d_vec, w_r, w_k, w_v, mu_r, mu_k, out):
    xs = nc.dram_tensor("xs_scratch", (BATCH, SEQ, DM), F32).ap()
    x2 = nc.dram_tensor("x2_scratch", (BATCH, SEQ, DM), F32).ap()
    hT_pad = nc.dram_tensor("hT_scratch", (P, NB, BATCH * ROW + TAIL), F32).ap()
    bc_dram = nc.dram_tensor("bc_scratch", (2 * DS, T), F32).ap()
    ffn_phase(nc, "f1", inp, w_r, w_k, w_v, mu_r, mu_k, xs, hT_pad)
    mixer_phase(nc, hT_pad, xs, w_in, conv_w, conv_b, w_x, w_dt, b_dt, w_out, a_mat, d_vec, bc_dram, x2)
    ffn_phase(nc, "f2", x2, w_r, w_k, w_v, mu_r, mu_k, out)


_INS = ["L0_attn_inp", "L0_attn_W_in", "L0_attn_conv_w", "L0_attn_conv_b", "L0_attn_W_x", "L0_attn_W_dt",
        "L0_attn_b_dt", "L0_attn_W_out", "L0_attn_A", "L0_attn_D", "L0_ffn_W_r", "L0_ffn_W_k", "L0_ffn_W_v",
        "L0_ffn_mu_r", "L0_ffn_mu_k"]


def kernel(**inputs):
    import numpy as np
    import concourse.bacc as bacc
    from concourse.bass_utils import run_bass_kernel_spmd

    nc = bacc.Bacc("TRN2", target_bir_lowering=False, num_devices=1)
    arrays, args = {}, []
    for name in _INS:
        a = np.ascontiguousarray(inputs[name])
        arrays[f"in_{name}"] = a
        args.append(nc.dram_tensor(f"in_{name}", a.shape, mybir.dt.from_np(a.dtype), kind="ExternalInput").ap())
    args.append(nc.dram_tensor("out_dram", (BATCH, SEQ, DM), F32, kind="ExternalOutput").ap())
    program(nc, *args)
    r = run_bass_kernel_spmd(nc, [arrays], core_ids=[0])
    return r.results[0]["out_dram"]
```

```python
from contextlib import ExitStack

import concourse.bass as bass
from concourse import mybir

F32 = mybir.dt.float32
F32R = mybir.dt.float32r
ALU = mybir.AluOpType
ACT = mybir.ActivationFunctionType

P = 128
BATCH, SEQ, DM = 4, 2048, 512
DI, DS, KC = 1024, 16, 4
EPS = 1e-5
NB = DM // P
ND = DI // P
PAD_L, PAD_R = 1, 2

FT = 512
FJ = FT // P
FC = SEQ // FT
NX = FC

T = 256
TJ = T // P
TH = T + PAD_L + PAD_R
MC = SEQ // T
SG = 4
NG = DS // SG
NU = NG * ND
NH = 8
NM = 2
NL = 4
NA = 2
NP = 4
ROW = SEQ + PAD_L + PAD_R
TAIL = T + TH


def ffn_phase(nc, name, x_in, w_r, w_k, w_v, mu_r, mu_k, out, hT_pad=None):
    mixer = hT_pad is not None
    x_v = x_in.rearrange("b (c j p) d -> (b c) p j d", c=FC, p=P)
    out_v = out.rearrange("b (c j p) d -> (b c) p j d", c=FC, p=P)

    with ExitStack() as ctx:
        def sb(n, shape, dt=F32):
            return ctx.enter_context(nc.sbuf_tensor(f"{name}_{n}", shape, dt))

        def sem(n):
            return ctx.enter_context(nc.semaphore(f"{name}_{n}"))

        ident = sb("ident", [P, P])
        w_hi = sb("w_hi", [P, 3, NB, DM], F32R)
        w_lo = sb("w_lo", [P, 3, NB, DM], F32R)
        mu = sb("mu", [P, 2, NB])
        half = sb("half", [P, FJ])
        x = sb("x", [P, NX, FJ, DM])
        stats = sb("stats", [P, FJ, 6])
        mv = sb("mv", [P, 2, FJ, 2])
        ve = sb("ve", [P, 2, FJ])
        rstd = sb("rstd", [P, 2, FJ])
        mark = sb("mark", [P, 1])
        hx = sb("hx", [P, FJ, DM])
        xhT = sb("xhT", [P, 2, NB, FT + 1])
        dsh = sb("dsh", [P, NB, FT])
        mix = sb("mix", [P, NB, FT])
        xr_hi = sb("xr_hi", [P, NB, FT], F32R)
        xr_lo = sb("xr_lo", [P, NB, FT], F32R)
        xk_hi = sb("xk_hi", [P, NB, FT], F32R)
        xk_lo = sb("xk_lo", [P, NB, FT], F32R)
        ka = sb("ka", [P, NB, FT])
        ka_hi = sb("ka_hi", [P, NB, FT], F32R)
        ka_lo = sb("ka_lo", [P, NB, FT], F32R)
        rt = sb("rt", [P, FJ, DM])
        h2 = sb("h2", [P, FJ, DM]) if mixer else None
        h2T = sb("h2T", [P, NB, TAIL]) if mixer else None
        zpad = h2T
        w_nat = (rt[:, :, :], ka[:, :, :], x[:, NX - 1])

        ps_kr = [ctx.enter_context(nc.psum_tensor(f"{name}_ps_kr{n}", [P, 512], F32)) for n in range(2)]
        ps_v = [ctx.enter_context(nc.psum_tensor(f"{name}_ps_v{n}", [P, 512], F32)) for n in range(FJ)]
        ps_t = [ctx.enter_context(nc.psum_tensor(f"{name}_ps_t{n}", [P, 512], F32)) for n in range(2)]

        s_id = sem("ident_made")
        s_w = sem("weights_loaded")
        s_x = [sem(f"x_loaded{n}") for n in range(NX)]
        s_wt = sem("weight_transposed")
        s_wh = sem("weight_high_ready")
        s_wc = sem("weight_split")
        s_st = sem("ln_chain")
        s_ve = sem("variance_ready")
        s_rs = sem("rstd_ready")
        s_hx = sem("hx_ready")
        s_t = sem("transposed")
        s_tc = sem("xhT_ready")
        s_prev = sem("prev_column_ready")
        s_dsh = sem("dsh_ready")
        s_mk = sem("xk_mixed")
        s_mr = sem("xr_mixed")
        s_hi = sem("mix_high_ready")
        s_xk = sem("xk_ready")
        s_xr = sem("xr_ready")
        s_kr = sem("kr_in_psum")
        s_kre = sem("kr_evacuated")
        s_sq = sem("relu_squared")
        s_relu = sem("ka_high_ready")
        s_ka = sem("ka_ready")
        s_v = sem("v_in_psum")
        s_vt = sem("v_used")
        s_x1 = sem("x1_ready")
        s_h2 = sem("h2_ready")
        s_xs = sem("xs_ready")
        s_t2 = sem("h2_transposed")
        s_t2c = sem("h2T_ready")
        s_pad = sem("pad_zeroed")
        s_out = sem("out_stored")
        s_ht = sem("hT_stored")
        block = ctx.enter_context(nc.Block())

        def over_chunks(eng, prologue, body):
            if prologue:
                prologue()
            with eng.Fori(0, BATCH - 1) as b:
                for c in range(FC):
                    body(b, c, FC * b + c, 0)
            for c in range(FC):
                body(BATCH - 1, c, FC * (BATCH - 1) + c, FC - c)


        def norms_before_2(i, left):
            return 2 * i + 3 - {1: 2, 2: 1}.get(left, 0)

        @block.sync
        def _(sp):
            sp.dma_start(x[:, 0], x_v[0]).then_inc(s_x[0], 16)
            for n, w in enumerate((w_r, w_k, w_v)):
                sp.dma_start(w_nat[n], w.rearrange("(o p) c -> p o c", p=P)).then_inc(s_w, 16)
            for n, m in enumerate((mu_r, mu_k)):
                sp.dma_start(mu[:, n, :], m.rearrange("(o p) -> p o", p=P),
                             allow_slow_non_contiguous=True).then_inc(s_w, 16)
            for c in range(1, NX):
                if c == NX - 1:
                    sp.wait_ge(s_wt, 3 * NB)
                sp.dma_start(x[:, c], x_v[c]).then_inc(s_x[c], 16)
            if mixer:
                sp.wait_ge(s_pad, 1)
                for b in range(BATCH):
                    sp.dma_start(hT_pad[:, :, b * ROW:b * ROW + PAD_L], zpad[:, :, 0:PAD_L],
                                 allow_slow_non_contiguous=True).then_inc(s_ht, 16)
                    sp.dma_start(hT_pad[:, :, (b + 1) * ROW - PAD_R:(b + 1) * ROW], zpad[:, :, 0:PAD_R]).then_inc(s_ht, 16)
                sp.dma_start(hT_pad[:, :, BATCH * ROW:], zpad[:, :, :]).then_inc(s_ht, 16)
            pads = (2 * BATCH + 1) * 16 if mixer else 0

            def body(b, c, i, left):
                sp.wait_ge(s_xs if mixer else s_x1, i + 1)
                sp.dma_start(out_v[i], x[:, c]).then_inc(s_out, 16)
                if left == 0:
                    sp.wait_ge(s_out, 16 * (i + 1))
                    sp.dma_start(x[:, c], x_v[i + NX]).then_inc(s_x[c], 16)
                if mixer:
                    sp.wait_ge(s_t2c, NB * (i + 1))
                    sp.dma_start(hT_pad[:, :, bass.ds(ROW * b + PAD_L + c * FT, FT)], h2T[:, :, 0:FT]).then_inc(s_ht, 16)

            over_chunks(sp, None, body)
            sp.wait_ge(s_out, 16 * BATCH * FC)
            if mixer:
                sp.wait_ge(s_ht, pads + 16 * BATCH * FC)

        @block.gpsimd
        def _(pool):
            nc.gpsimd.memset(ident[:, :], 0.0).then_inc(s_id, 1)
            nc.gpsimd.memset(half[:, :], -0.5).then_inc(s_id, 1)
            pool.wait_ge(s_id, 2)
            nc.gpsimd.affine_select(out=ident[:, :], in_=ident[:, :], compare_op=ALU.not_equal, fill=1.0,
                                    base=0, pattern=[[-1, P]], channel_multiplier=1).then_inc(s_id, 1)
            if mixer:
                nc.gpsimd.memset(zpad[:, :, :], 0.0).then_inc(s_pad, 1)
            def power(which, k):
                pool.wait_ge(s_ve, k + 1)
                nc.gpsimd.tensor_tensor(rstd[:, which], ve[:, which], half[:, :], ALU.pow).then_inc(s_rs, 1)

            def shift(i, slot):
                pool.wait_ge(s_tc, NB * (i + 1))
                pool.wait_ge(s_prev, i + 1)
                if not (isinstance(i, int) and i == 0):
                    pool.wait_ge(s_xr, i)
                nc.gpsimd.tensor_tensor(dsh[:, :, :], xhT[:, slot, :, 1:FT + 1], xhT[:, slot, :, 0:FT],
                                        ALU.subtract).then_inc(s_dsh, 1)

            def prologue():
                power(0, 0)
                shift(0, 0)
                power(0, 1)
                shift(1, 1)
                power(0, 2)

            def body(b, c, i, left):
                if left == 0 or left > 2:
                    shift(i + 2, c % 2)
                if mixer:
                    power(1, norms_before_2(i, left))
                    pool.wait_ge(s_h2, FJ * (i + 1))
                    nc.gpsimd.tensor_tensor(x[:, c], x[:, c], h2[:, :, :], ALU.add).then_inc(s_xs, 1)
                if left == 0 or left > 3:
                    power(0, norms_before_2(i, left) + 1 if mixer else i + 3)

            over_chunks(pool, prologue, body)

        @block.scalar
        def _(act):
            def copy_weights():
                for g in range(3 * NB):
                    act.wait_ge(s_wt, g + 1)
                    nc.scalar.activation(w_hi[:, g // NB, g % NB, :], ps_t[g % 2][:, :], ACT.Copy).then_inc(s_wh, 1)

            def copy_xhT(i, slot, seq_start):
                if not (isinstance(i, int) and i < 2):
                    act.wait_ge(s_xr, i - 1)
                if seq_start:
                    nc.scalar.activation(xhT[:, slot, :, 0], ident[:, 0:NB], ACT.Copy, scale=0.0).then_inc(s_prev, 1)
                else:
                    act.wait_ge(s_tc, NB * i)
                    nc.scalar.activation(xhT[:, slot, :, 0], xhT[:, 1 - slot, :, FT], ACT.Copy).then_inc(s_prev, 1)
                for f in range(NB):
                    act.wait_ge(s_t, NB * i + f + 1)
                    nc.scalar.activation(xhT[:, slot, f, 1:FT + 1], ps_t[f % 2][:, :], ACT.Copy).then_inc(s_tc, 1)

            def high_xk(i):
                if not (isinstance(i, int) and i == 0):
                    act.wait_ge(s_kr, 2 * NB * i - NB)
                act.wait_ge(s_mk, NB * (i + 1))
                nc.scalar.activation(xk_hi[:, :, :], mix[:, :, :], ACT.Copy).then_inc(s_hi, 1)

            def high_xr(i):
                if not (isinstance(i, int) and i == 0):
                    act.wait_ge(s_kr, 2 * NB * i)
                act.wait_ge(s_mr, NB * (i + 1))
                nc.scalar.activation(xr_hi[:, :, :], mix[:, :, :], ACT.Copy).then_inc(s_hi, 1)

            def copy_k(i):
                for d in range(NB):
                    act.wait_ge(s_kr, 2 * NB * i + d + 1)
                    nc.scalar.activation(ka[:, d, :], ps_kr[d % 2][:, :], ACT.Relu).then_inc(s_kre, 1)
                    act.wait_ge(s_kre, 2 * NB * i + d + 1)
                    nc.scalar.activation(ka[:, d, :], ka[:, d, :], ACT.Square).then_inc(s_sq, 1)
                    act.wait_ge(s_sq, NB * i + d + 1)
                    nc.scalar.activation(ka_hi[:, d, :], ka[:, d, :], ACT.Copy).then_inc(s_relu, 1)

            def copy_r(i, tiles):
                if not (isinstance(i, int) and i == 0):
                    act.wait_ge(s_x1, i)
                for j in tiles:
                    act.wait_ge(s_kr, 2 * NB * i + NB + j + 1)
                    nc.scalar.activation(rt[:, j, :], ps_kr[j % 2][:, :], ACT.Tanh, scale=0.5).then_inc(s_kre, 1)

            def prologue():
                act.wait_ge(s_id, 3)
                copy_xhT(0, 0, True)
                copy_weights()
                high_xk(0)
                high_xr(0)
                copy_k(0)
                copy_xhT(1, 1, False)
                high_xk(1)
                copy_r(0, range(FJ))
                high_xr(1)

            def body(b, c, i, left):
                if left == 0 or left > 2:
                    copy_xhT(i + 2, c % 2, c + 2 == FC)
                if left == 0 or left > 1:
                    copy_k(i + 1)
                if left == 0 or left > 1:
                    copy_r(i + 1, range(2))
                if left == 0 or left > 2:
                    high_xk(i + 2)
                if left == 0 or left > 1:
                    copy_r(i + 1, range(2, FJ))
                if mixer:
                    act.wait_ge(s_ht, (2 * BATCH + 1) * 16 + 16 * i)
                    for f in range(NB):
                        act.wait_ge(s_t2, NB * i + f + 1)
                        nc.scalar.activation(h2T[:, f, 0:FT], ps_t[f % 2][:, :], ACT.Copy).then_inc(s_t2c, 1)
                if left == 0 or left > 2:
                    high_xr(i + 2)

            over_chunks(act, prologue, body)

        @block.vector
        def _(dve):
            V = nc.vector
            def norm(which, src, dst, k, done, before):
                st = 2 * FJ * k
                for j in range(FJ):
                    V.bn_stats(out=stats[:, j, :], in_=src[:, j, :]).then_inc(s_st, 1)
                dve.wait_ge(s_st, st + FJ)
                V.memset(mark[:, :], 0.0)
                for j in range(FJ):
                    V.bn_aggr(out=mv[:, which, j, :], in_=stats[:, j, :]).then_inc(s_st, 1)
                dve.wait_ge(s_st, st + 2 * FJ)
                V.tensor_scalar(ve[:, which], mv[:, which, :, 1], EPS, None, ALU.add).then_inc(s_ve, 1)
                dve.wait_ge(s_rs, k + 1)
                before()
                for j in range(FJ):
                    V.tensor_scalar(dst[:, j, :], src[:, j, :], mv[:, which, j, 0:1], rstd[:, which, j:j + 1],
                                    ALU.subtract, ALU.mult).then_inc(done, 1)

            def norm1(i, slot, k, nth):
                dve.wait_ge(s_x[slot], 16 * nth)

                def free():
                    if not (isinstance(i, int) and i == 0):
                        dve.wait_ge(s_t, NB * i)
                norm(0, x[:, slot], hx, k, s_hx, free)

            def mixed(i, slot, n, lo, hi, done, low):
                dve.wait_ge(s_dsh, i + 1)
                if n == 0:
                    dve.wait_ge(s_xk, i + 1)
                elif not (isinstance(i, int) and i == 0):
                    dve.wait_ge(s_xr, i)
                for f in range(NB):
                    V.scalar_tensor_tensor(out=mix[:, f, :], in0=dsh[:, f, :], scalar=mu[:, n, f:f + 1],
                                           in1=xhT[:, slot, f, 0:FT], op0=ALU.mult, op1=ALU.add).then_inc(done, 1)
                dve.wait_ge(s_hi, 2 * i + 2 - n)
                V.tensor_tensor(lo[:, :, :], mix[:, :, :], hi[:, :, :].bitcast(F32), ALU.subtract).then_inc(low, 1)

            def mixed_k(i, slot):
                mixed(i, slot, 1, xk_lo, xk_hi, s_mk, s_xk)

            def mixed_r(i, slot):
                mixed(i, slot, 0, xr_lo, xr_hi, s_mr, s_xr)

            def split_k(i):
                for d in range(NB):
                    dve.wait_ge(s_relu, NB * i + d + 1)
                    V.tensor_tensor(ka_lo[:, d, :], ka[:, d, :], ka_hi[:, d, :].bitcast(F32),
                                    ALU.subtract).then_inc(s_ka, 1)

            norm1(0, 0, 0, 1)
            dve.wait_ge(s_w, 5 * 16)
            for g in range(3 * NB):
                dve.wait_ge(s_wh, g + 1)
                V.tensor_tensor(w_lo[:, g // NB, g % NB, :], ps_t[g % 2][:, :],
                                w_hi[:, g // NB, g % NB, :].bitcast(F32), ALU.subtract).then_inc(s_wc, 1)
            mixed_k(0, 0)
            mixed_r(0, 0)
            norm1(1, 1, 1, 1)
            split_k(0)
            mixed_k(1, 1)
            norm1(2, 2, 2, 1)
            mixed_r(1, 1)

            def body(b, c, i, left):
                for j in range(FJ):
                    dve.wait_ge(s_v, FJ * i + j + 1)
                    dve.wait_ge(s_kre, 2 * NB * i + NB + j + 1)
                    V.scalar_tensor_tensor(out=rt[:, j, :], in0=rt[:, j, :], scalar=1.0, in1=ps_v[j][:, :],
                                           op0=ALU.add, op1=ALU.mult).then_inc(s_vt, 1)
                dve.wait_ge(s_vt, FJ * (i + 1))
                for j in range(FJ):
                    ins = V.scalar_tensor_tensor(out=x[:, c, j, :], in0=rt[:, j, :], scalar=0.25,
                                                 in1=x[:, c, j, :], op0=ALU.mult, op1=ALU.add)
                ins.then_inc(s_x1, 1)
                if mixer:
                    dve.wait_ge(s_x1, i + 1)

                    def free():
                        if left in (1, 2):
                            dve.wait_ge(s_t2, NB * i)
                            dve.wait_ge(s_xs, i)
                    norm(1, x[:, c], h2, norms_before_2(i, left), s_h2, free)
                if left == 0 or left > 1:
                    split_k(i + 1)
                if left == 0 or left > 2:
                    mixed_k(i + 2, c % 2)
                if left == 0 or left > 3:
                    nth = (b if c + 3 < FC else b + 1) + 1
                    norm1(i + 3, (c + 3) % NX, norms_before_2(i, left) + 1 if mixer else i + 3, nth)
                if left == 0 or left > 2:
                    mixed_r(i + 2, c % 2)

            over_chunks(dve, None, body)

        @block.tensor
        def _(pe):
            M = nc.tensor

            def turn_weights():
                for g in range(3 * NB):
                    if g >= 2:
                        pe.wait_ge(s_wc, g - 1)
                    else:
                        pe.wait_ge(s_tc, NB)
                    for o in range(NB):
                        ins = M.transpose(ps_t[g % 2][:, o * P:(o + 1) * P],
                                          w_nat[g // NB][:, o, (g % NB) * P:(g % NB + 1) * P], ident[:, :])
                    ins.then_inc(s_wt, 1)

            def turn(i, src, ready, done, copied_before):
                pe.wait_ge(ready, FJ * (i + 1))
                for f in range(NB):
                    copied_before(f)
                    for j in range(FJ):
                        ins = M.transpose(ps_t[f % 2][:, j * P:(j + 1) * P], src[:, j, f * P:(f + 1) * P], ident[:, :])
                    ins.then_inc(done, 1)

            def turn1(i):
                def bank(f):
                    if f >= 2:
                        pe.wait_ge(s_tc, NB * i + f - 1)
                    elif mixer and not (isinstance(i, int) and i < 3):
                        pe.wait_ge(s_t2c, NB * (i - 2))
                    elif not (isinstance(i, int) and i == 0):
                        pe.wait_ge(s_tc, NB * i)
                turn(i, hx, s_hx, s_t, bank)

            def turn2(i):
                def bank(f):
                    if f >= 2:
                        pe.wait_ge(s_t2c, NB * i + f - 1)
                    elif isinstance(i, int) and i >= BATCH * FC - 2:
                        pe.wait_ge(s_tc, NB * BATCH * FC)
                        if i == BATCH * FC - 1:
                            pe.wait_ge(s_t2c, NB * i)
                    else:
                        pe.wait_ge(s_tc, NB * (i + 3))
                turn(i, h2, s_h2, s_t2, bank)

            def bank_free(n, first):
                if not (first and n < 2):
                    pe.wait_ge(s_kre, n - 1)

            def split_product(ps, terms):
                last = len(terms) - 1
                for n, (a_hi, a_lo, b_hi, b_lo) in enumerate(terms):
                    M.matmul(ps, a_hi, b_lo, start=(n == 0), stop=False)
                    M.matmul(ps, a_hi, b_hi, start=False, stop=False)
                    ins = M.matmul(ps, a_lo, b_hi, start=False, stop=(n == last))
                return ins

            def k_products(i):
                pe.wait_ge(s_xk, i + 1)
                for d in range(NB):
                    bank_free(2 * NB * i + d, isinstance(i, int) and i == 0 and d < 2)
                    o = slice(d * P, (d + 1) * P)
                    ins = split_product(ps_kr[d % 2][:, :], [
                        (w_hi[:, 1, f, o], w_lo[:, 1, f, o], xk_hi[:, f, :], xk_lo[:, f, :]) for f in range(NB)])
                    ins.then_inc(s_kr, 1)

            def r_products(i):
                pe.wait_ge(s_xr, i + 1)
                for j in range(FJ):
                    bank_free(2 * NB * i + NB + j, False)
                    t = slice(j * P, (j + 1) * P)
                    ins = split_product(ps_kr[j % 2][:, :], [
                        (xr_hi[:, f, t], xr_lo[:, f, t], w_hi[:, 0, f, :], w_lo[:, 0, f, :]) for f in range(NB)])
                    ins.then_inc(s_kr, 1)

            def v_products(i, c):
                pe.wait_ge(s_ka, NB * (i + 1))
                if c == 0:
                    pe.wait_ge(s_xk, i + 2)
                else:
                    pe.wait_ge(s_vt, FJ * i)
                for j in range(FJ):
                    t = slice(j * P, (j + 1) * P)
                    ins = split_product(ps_v[j][:, :], [
                        (ka_hi[:, d, t], ka_lo[:, d, t], w_hi[:, 2, d, :], w_lo[:, 2, d, :]) for d in range(NB)])
                    ins.then_inc(s_v, 1)

            def prologue():
                pe.wait_ge(s_id, 3)
                turn1(0)
                pe.wait_ge(s_w, 5 * 16)
                turn_weights()
                k_products(0)
                turn1(1)
                r_products(0)

            def body(b, c, i, left):
                v_products(i, c)
                if left == 0 or left > 2:
                    turn1(i + 2)
                if left == 0 or left > 1:
                    k_products(i + 1)
                    r_products(i + 1)
                if mixer:
                    turn2(i)

            over_chunks(pe, prologue, body)


def bcast(ap, n):
    return ap.unsqueeze(1).to_broadcast([ap.shape[0], n, ap.shape[1]])


def mixer_phase(nc, hT_pad, xs_in, w_in, conv_w, conv_b, w_x, w_dt, b_dt, w_out, a_mat, d_vec, bc_dram, out):
    xs_v = xs_in.rearrange("b (c j p) d -> (b c) p j d", c=MC, p=P)
    out_v = out.rearrange("b (c j p) d -> (b c) p j d", c=MC, p=P)
    LAST = BATCH * MC - 1

    with ExitStack() as ctx:
        def sb(n, shape):
            return ctx.enter_context(nc.sbuf_tensor(f"mx_{n}", shape, F32))

        def sem(n):
            return ctx.enter_context(nc.semaphore(f"mx_{n}"))

        ident = sb("ident", [P, P])
        w_in_sb = sb("w_in", [P, NB, 2 * DI])
        w_x_sb = sb("w_x", [P, ND, 2 * DS])
        w_dt_sb = sb("w_dt", [P, ND, DI])
        w_out_sb = sb("w_out", [P, ND, DM])
        cw = sb("cw", [P, KC, ND])
        cb = sb("cb", [P, ND])
        bdt = sb("bdt", [P, ND])
        a_sb = sb("a", [P, ND, DS])
        d_sb = sb("d", [P, ND])
        hst = sb("hst", [P, ND, DS])
        hT = sb("hT", [P, 2, NB, TH])
        u = sb("u", [P, 2, ND, T])
        ct = sb("ct", [P, 2, T])
        en = sb("en", [P, 2, T])
        dl = sb("dl", [P, NL, T])
        du = sb("du", [P, 2, T])
        zs = sb("zs", [P, 2, T])
        gy = sb("gy", [P, 2, T])
        bs = sb("bs", [P, NG, SG, T])
        cs = sb("cs", [P, NG, SG, T])
        bc = sb("bc", [2 * DS, T])
        da = sb("da", [P, NA, SG, T])
        dbu = sb("dbu", [P, NM, SG, T])
        hp = sb("hp", [P, NH, SG, T])
        xo = sb("xo", [P, TJ, DM])

        ps_y = [ctx.enter_context(nc.psum_tensor(f"mx_ps_y{n}", [P, 512], F32)) for n in range(2)]
        ps_o = [ctx.enter_context(nc.psum_tensor(f"mx_ps_o{n}", [P, DM], F32)) for n in range(TJ)]
        ps_m = [ctx.enter_context(nc.psum_tensor(f"mx_ps_m{n}", [P, 512], F32)) for n in range(NP)]

        s_id = sem("ident_made")
        s_w = [sem(f"w_in_loaded{n}") for n in range(2)]
        s_wv = sem("vectors_loaded")
        s_wp = sem("weights_loaded")
        s_mean = sem("w_in_mean")
        s_cen = sem("w_in_centred")
        s_prep = sem("weights_scaled")
        s_ht = [sem(f"hT_loaded{n}") for n in range(2)]
        s_pi = sem("input_in_psum")
        s_pz = sem("gate_in_psum")
        s_pb = sem("bc_in_psum")
        s_pd = sem("dt_in_psum")
        s_po = sem("out_blocks_summed")
        s_c0 = sem("conv_tap0")
        s_cv = sem("conv_steps")
        s_cq = sem("conv_ready")
        s_ct = sem("conv_tanh")
        s_u = sem("u_ready")
        s_bc = sem("bc_copied")
        s_bcd = sem("bc_stored")
        s_bl = [sem(f"b_loaded{n}") for n in range(NG)]
        s_cl = [sem(f"c_loaded{n}") for n in range(NG)]
        s_abs = sem("dt_abs")
        s_rl = sem("dt_relu")
        s_en = sem("dt_exp")
        s_sp = sem("dt_log")
        s_dl = sem("delta_ready")
        s_du = sem("du_ready")
        s_m1 = sem("dbu_ready")
        s_da = sem("da_ready")
        s_sc = sem("scanned")
        s_m2 = sem("hc_ready")
        s_pr = sem("pairs_added")
        s_r = sem("states_summed")
        s_st = sem("state_kept")
        s_zt = sem("z_tanh")
        s_zs = sem("zs_ready")
        s_yd = sem("yd_ready")
        s_g = sem("gated")
        s_x = sem("xs_loaded")
        s_o = sem("out_ready")
        s_out = sem("out_stored")
        s_rst = sem("state_zeroed")
        block = ctx.enter_context(nc.Block())

        mean_w = hp[:, 0, 0, 0:P]

        AT = {
            "in": [n - NU for n in (0, 2, 5, 7, 10, 12, 15, 17)],
            "bc": [27 - NU],
            "dt": [NG * b - 2 * NG - 2 for b in range(ND)],
            "gate": [NG * b + 1 for b in range(ND)],
        }
        AT["dt0"] = [n - 1 for n in AT["dt"]]
        DT_EARLY = 4
        YG_AT = [NG * b + NG + 4 for b in range(ND)]
        OUT_AT = [n + 2 for n in YG_AT]
        EVAC_AT = [OUT_AT[-1] + 1]
        TAP, TANH, SILU = 2, 3, 3
        GATE, COPY = 2, 2
        RELU, EXP, ADD = 2, 2, 0
        LOG_AT = [AT["dt"][b] + 3 for b in range(1, ND, 2)]
        PAIR_LAG, SUM_LAG = 3, 4

        PAIRED = [n % NG != 0 for n in range(NU)]

        def due(units, n, i, lag=0):
            shifts = (1, 0) if is0(i) else (1, 0, -1)
            return [(b, s) for s in shifts for b, at in enumerate(units) if at + lag == n - NU * s]

        def is0(i):
            return isinstance(i, int) and i == 0

        order = []
        for n in range(NU):
            for kind, units in (("bc", "bc"), ("gate", "gate"), ("in", "in"), ("dt", "dt0")):
                order += [(kind, b, s) for b, s in due(AT[units], n, 0)]
        order.append(("skip", 0, 0))
        first_order = [(kind, b) for kind, units in (("in", "in"), ("bc", "bc"), ("dt", "dt0"))
                       for b, at in enumerate(AT[units]) if at < 0]

        def shift(kind, b):
            return 1 if AT["dt0" if kind == "dt" else kind][b] < 0 else 0

        def bank(kind, b, c, cp):
            s = shift(kind, b)
            if is0(c) and s:
                return ps_m[first_order.index((kind, b)) % NP]
            return ps_m[(len(first_order) + len(order) * ((cp - s) % 2) + order.index((kind, b, s))) % NP]

        def over_chunks(eng, prologue, body, sequence=None, epilogue=None):
            if prologue:
                prologue()
            if sequence:
                sequence(0)
            body(0, 0)
            body(1, 1)
            with eng.Fori(1, MC // 2) as c2:
                for par in range(2):
                    body(2 * c2 + par, par)
            with eng.Fori(1, BATCH) as b:
                if sequence:
                    sequence(b)
                with eng.Fori(0, MC // 2) as c2:
                    for par in range(2):
                        body(MC * b + 2 * c2 + par, par)
            if epilogue:
                epilogue()

        @block.sync
        def _(sp):
            def load_hT(b, c, par):
                sp.dma_start(hT[:, par], hT_pad[:, :, bass.ds(ROW * b + T * c, TH)]).then_inc(s_ht[par], 16)

            def spread(g, dst, done, first):
                rows = bc_dram[first + SG * g:first + SG * (g + 1), :].rearrange("s t -> (s t)")
                sp.dma_start(dst[:, g].rearrange("p s t -> p (s t)"),
                             rows.unsqueeze(0).to_broadcast([P, SG * T])).then_inc(done[g], 16)

            def store_bc(i):
                sp.wait_ge(s_bc, 16 * (i + 1))
                sp.dma_start(bc_dram[:, :], bc[:, :]).then_inc(s_bcd, 16)
                sp.wait_ge(s_bcd, 16 * (i + 1))

            def chunk(i, par, b_next, c_next):
                if not is0(i):
                    sp.wait_ge(s_out, 16 * i)
                sp.dma_start(xo[:, :, :], xs_v[i]).then_inc(s_x, 16)
                store_bc(i + 1)
                for g in range(NG):
                    sp.wait_ge(s_m1, NU * i + NU - NG + g + 1)
                    spread(g, bs, s_bl, 0)
                    sp.wait_ge(s_m2, NU * i + NU - NG + g + 1)
                    spread(g, cs, s_cl, DS)
                    if g == 0:
                        sp.wait_ge(s_pz, ND * (i + 1))
                        load_hT(b_next, c_next, par)
                sp.wait_ge(s_o, i + 1)
                sp.dma_start(out_v[i], xo[:, :, :]).then_inc(s_out, 16)

            for half in range(2):
                columns = slice(half * DI, (half + 1) * DI)
                sp.dma_start(w_in_sb[:, :, columns], w_in[:, columns].rearrange("(f p) n -> p f n", p=P)).then_inc(s_w[half], 16)
            for dst, src in (
                (cw[:, :, :], conv_w.rearrange("k o (f p) -> p (k o) f", p=P)),
                (cb[:, :], conv_b.rearrange("(f p) -> p f", p=P)),
                (bdt[:, :], b_dt.rearrange("(f p) -> p f", p=P)),
                (d_sb[:, :], d_vec.rearrange("(f p) -> p f", p=P)),
                (a_sb[:, :, :], a_mat.rearrange("(f p) n -> p f n", p=P)),
            ):
                sp.dma_start(dst, src, allow_slow_non_contiguous=True).then_inc(s_wv, 16)
            load_hT(0, 0, 0)
            for dst, src in ((w_x_sb, w_x), (w_dt_sb, w_dt), (w_out_sb, w_out)):
                sp.dma_start(dst[:, :, :], src.rearrange("(f p) n -> p f n", p=P)).then_inc(s_wp, 16)
            load_hT(0, 1, 1)
            store_bc(0)
            for g in range(NG):
                spread(g, bs, s_bl, 0)
                spread(g, cs, s_cl, DS)

            def last_pair(b):
                for par in range(2):
                    chunk(MC * b + MC - 2 + par, par, b + 1, par)

            for par in range(2):
                chunk(par, par, 0, 2 + par)
            with sp.Fori(1, MC // 2 - 1) as c2:
                for par in range(2):
                    chunk(2 * c2 + par, par, 0, 2 * c2 + 2 + par)
            last_pair(0)
            with sp.Fori(1, BATCH) as b:
                with sp.Fori(0, MC // 2 - 1) as c2:
                    for par in range(2):
                        chunk(MC * b + 2 * c2 + par, par, b, 2 * c2 + 2 + par)
                last_pair(b)
            sp.wait_ge(s_out, 16 * (LAST + 1))

        @block.gpsimd
        def _(pool):
            G = nc.gpsimd
            G.memset(ident[:, :], 0.0).then_inc(s_id, 1)
            G.memset(mean_w, 1.0 / DM).then_inc(s_id, 1)
            pool.wait_ge(s_id, 2)
            G.affine_select(out=ident[:, :], in_=ident[:, :], compare_op=ALU.not_equal, fill=1.0,
                            base=0, pattern=[[-1, P]], channel_multiplier=1).then_inc(s_id, 1)

            def pairs(c, n):
                if PAIRED[n]:
                    k = n % NH
                    pool.wait_ge(s_m2, NU * c + n + 1)
                    G.tensor_tensor(hp[:, k, 0:2, :], hp[:, k, 0:2, :], hp[:, k, 2:4, :], ALU.add).then_inc(s_pr, 1)

            def body(i, par):
                for n in range(NU):
                    b, g = divmod(n, NG)
                    if g == 0:
                        pool.wait_ge(s_dl, ND * i + b + 1)
                        G.tensor_tensor(du[:, b % 2, :], dl[:, b % NL, :], u[:, par, b, :], ALU.mult).then_inc(s_du, 1)
                    if b == 0:
                        pool.wait_ge(s_bl[g], 16 * (i + 1))
                    if g == 0:
                        pool.wait_ge(s_du, ND * i + b + 1)
                    if not (is0(i) and n < NM):
                        pool.wait_ge(s_sc, 2 * NU * i + 2 * (n - NM + 1))
                    G.tensor_tensor(dbu[:, n % NM], bs[:, g], bcast(du[:, b % 2, :], SG), ALU.mult).then_inc(s_m1, 1)
                    if n >= PAIR_LAG:
                        pairs(i, n - PAIR_LAG)
                    elif not is0(i):
                        pairs(i - 1, NU + n - PAIR_LAG)

            over_chunks(pool, None, body, None, lambda: [pairs(LAST, n) for n in range(NU - PAIR_LAG, NU)])

        @block.scalar
        def _(act):
            A = nc.scalar

            def tap0(c, cp, b):
                act.wait_ge(s_pi, ND * c + b + 1)
                A.activation(u[:, cp, b, :], bank("in", b, c, cp)[:, 0:T], ACT.Identity, scale=cw[:, 0, b:b + 1],
                             bias=cb[:, b:b + 1]).then_inc(s_c0, 1)

            def conv_tanh(c, cp, b):
                act.wait_ge(s_cq, ND * c + b + 1)
                if b >= 2 or not is0(c):
                    act.wait_ge(s_u, ND * c + b - 1)
                A.activation(ct[:, b % 2, :], u[:, cp, b, :], ACT.Tanh).then_inc(s_ct, 1)

            def copy_bc(c, cp):
                act.wait_ge(s_pb, c + 1)
                if not is0(c):
                    act.wait_ge(s_bcd, 16 * c)
                A.activation(bc[:, :], bank("bc", 0, c, cp)[0:2 * DS, 0:T], ACT.Copy).then_inc(s_bc, 16)

            def relu(c, cp, b):
                ps = bank("dt", b, c, cp)[:, 0:T]
                act.wait_ge(s_pd, ND * c + b + 1)
                if b % 2 == 0 and not (is0(c) and b == 0):
                    act.wait_ge(s_dl, ND * c + b)
                A.activation(en[:, b % 2, :], ps, ACT.Abs, bias=bdt[:, b:b + 1]).then_inc(s_abs, 1)
                A.activation(dl[:, b % NL, :], ps, ACT.Relu, bias=bdt[:, b:b + 1]).then_inc(s_rl, 1)

            def exp_neg(c, b):
                act.wait_ge(s_abs, ND * c + b + 1)
                A.activation(en[:, b % 2, :], en[:, b % 2, :], ACT.Exp, scale=-1.0).then_inc(s_en, 1)

            def log(c, pair):
                act.wait_ge(s_en, ND * c + 2 * pair + 2)
                A.activation(en[:, :, :], en[:, :, :], ACT.Ln, bias=1.0).then_inc(s_sp, 1)

            def gate_tanh(c, cp, b):
                act.wait_ge(s_pz, ND * c + b + 1)
                if b >= 2 or not is0(c):
                    act.wait_ge(s_g, ND * c + b - 1)
                A.activation(zs[:, b % 2, :], bank("gate", b, c, cp)[:, 0:T], ACT.Tanh, scale=0.5).then_inc(s_zt, 1)

            def keep(c, n):
                b, g = divmod(n, NG)
                A.activation(hst[:, b, SG * g:SG * (g + 1)], hp[:, n % NH, :, T - 1], ACT.Copy).then_inc(s_st, 1)

            def prologue():
                act.wait_ge(s_wv, 16 * 5)
                act.wait_ge(s_prep, 2)
                for b in range(ND):
                    tap0(0, 0, b)
                    conv_tanh(0, 0, b)
                copy_bc(0, 0)
                A.preload_act_table_set("natural_log_exp_and_others")
                for b in range(ND):
                    if AT["dt"][b] + RELU < 0:
                        relu(0, 0, b)
                    if AT["dt"][b] + EXP < 0:
                        exp_neg(0, b)
                    if b % 2 and LOG_AT[b // 2] < 0:
                        log(0, b // 2)
                A.preload_act_table_set("exp_and_others")

            def body(i, par):
                for n in range(NU):
                    b, g = divmod(n, NG)
                    if g == 0:
                        act.wait_ge(s_dl, ND * i + b + 1)
                    for half in range(2):
                        if half == 0 and not (is0(i) and n < NA):
                            act.wait_ge(s_sc, 2 * NU * i + 2 * (n - NA + 1))
                            keep(i if n >= NA else i - 1, (n - NA) % NU)
                        for k in range(2):
                            s = SG * g + 2 * half + k
                            ins = A.activation(da[:, n % NA, s % SG, :], dl[:, b % NL, :], ACT.Exp, scale=a_sb[:, b, s:s + 1])
                        ins.then_inc(s_da, 1)
                        if half == 0:
                            for bb, s in due(AT["in"], n, i, TAP):
                                tap0(i + s, (par + s) % 2, bb)
                            for bb, s in due(AT["dt"], n, i, RELU):
                                relu(i + s, (par + s) % 2, bb)
                            for pair, s in due(LOG_AT, n, i):
                                A.preload_act_table_set("natural_log_exp_and_others")
                                log(i + s, pair)
                    if due(LOG_AT, n, i):
                        A.preload_act_table_set("exp_and_others")
                    for bb, s in due(AT["gate"], n, i, GATE):
                        gate_tanh(i + s, (par + s) % 2, bb)
                    for bb, s in due(AT["in"], n, i, TANH):
                        conv_tanh(i + s, (par + s) % 2, bb)
                    for bb, s in due(AT["bc"], n, i, COPY):
                        copy_bc(i + s, (par + s) % 2)
                    for bb, s in due(AT["dt"], n, i, EXP):
                        exp_neg(i + s, bb)

            def epilogue():
                for n in range(NU - NA, NU):
                    act.wait_ge(s_sc, 2 * (NU * LAST + n + 1))
                    keep(LAST, n)

            over_chunks(act, prologue, body, None, epilogue)

        @block.vector
        def _(dve):
            V = nc.vector

            def weights():
                dve.wait_ge(s_wv, 16 * 5)
                V.tensor_scalar(cw[:, :, :], cw[:, :, :], 0.5, None, ALU.mult).then_inc(s_prep, 1)
                V.tensor_scalar(cb[:, :], cb[:, :], 0.5, None, ALU.mult).then_inc(s_prep, 1)
                for c in range(2 * DI // 512):
                    dve.wait_ge(s_mean, c + 1)
                    for f in range(NB):
                        w = w_in_sb[:, f, 512 * c:512 * (c + 1)]
                        ins = V.tensor_tensor(w, w, ps_m[c % 2][:, :], ALU.subtract)
                    ins.then_inc(s_cen, 1)
                dve.wait_ge(s_prep, 2)

            def conv(c, cp, b, step):
                q = u[:, cp, b, :]
                if step == 1:
                    dve.wait_ge(s_c0, ND * c + b + 1)
                else:
                    dve.wait_ge(s_cv, (KC - 2) * (ND * c + b) + step - 1)
                V.scalar_tensor_tensor(out=q, in0=bank("in", b, c, cp)[:, step:step + T], scalar=cw[:, step, b:b + 1],
                                       in1=q, op0=ALU.mult, op1=ALU.add).then_inc(s_cq if step == KC - 1 else s_cv, 1)

            def silu(c, cp, b):
                dve.wait_ge(s_ct, ND * c + b + 1)
                q = u[:, cp, b, :]
                V.scalar_tensor_tensor(out=q, in0=ct[:, b % 2, :], scalar=1.0, in1=q,
                                       op0=ALU.add, op1=ALU.mult).then_inc(s_u, 1)

            def add_log(c, pair):
                d = dl[:, 2 * pair % NL:2 * pair % NL + 2, :]
                dve.wait_ge(s_sp, ND // 2 * c + pair + 1)
                V.tensor_tensor(d, d, en[:, :, :], ALU.add).then_inc(s_dl, 2)

            def gate(c, cp, b):
                dve.wait_ge(s_zt, ND * c + b + 1)
                z = zs[:, b % 2, :]
                V.scalar_tensor_tensor(out=z, in0=z, scalar=1.0, in1=bank("gate", b, c, cp)[:, 0:T],
                                       op0=ALU.add, op1=ALU.mult).then_inc(s_zs, 1)

            def gated(c, cp, b):
                y = gy[:, b % 2, :]
                dve.wait_ge(s_r, NU * c + NG * (b + 1))
                if b >= 2 or not is0(c):
                    dve.wait_ge(s_po, ND * c + b - 1)
                V.scalar_tensor_tensor(out=y, in0=u[:, cp, b, :], scalar=d_sb[:, b:b + 1],
                                       in1=ps_y[b % 2][:, 0:T], op0=ALU.mult, op1=ALU.add).then_inc(s_yd, 1)
                dve.wait_ge(s_zs, ND * c + b + 1)
                dve.wait_ge(s_yd, ND * c + b + 1)
                V.tensor_tensor(y, y, zs[:, b % 2, :], ALU.mult).then_inc(s_g, 1)

            def residual(c):
                dve.wait_ge(s_po, ND * (c + 1))
                dve.wait_ge(s_x, 16 * (c + 1))
                for j in range(TJ):
                    ins = V.tensor_tensor(xo[:, j, :], ps_o[j][:, :], xo[:, j, :], ALU.add)
                ins.then_inc(s_o, 1)

            def times_c(c, n):
                b, g = divmod(n, NG)
                if b == 0:
                    dve.wait_ge(s_cl[g], 16 * (c + 1))
                h = hp[:, n % NH]
                dve.wait_ge(s_st, NU * c + n + 1)
                V.tensor_tensor(h, h, cs[:, g], ALU.mult).then_inc(s_m2, 1)

            def scans(i, n, half):
                b, g = divmod(n, NG)
                dve.wait_ge(s_da, 2 * (NU * i + n) + half + 1)
                for k in range(2):
                    s = 2 * half + k
                    ins = V.tensor_tensor_scan(hp[:, n % NH, s, :], da[:, n % NA, s, :], dbu[:, n % NM, s, :],
                                               hst[:, b, SG * g + s:SG * g + s + 1], ALU.mult, ALU.add)
                ins.then_inc(s_sc, 1)

            def prologue():
                weights()
                for b in range(ND):
                    for step in range(1, KC):
                        conv(0, 0, b, step)
                    silu(0, 0, b)
                for pair, at in enumerate(LOG_AT):
                    if at + ADD < 0:
                        add_log(0, pair)
                dve.wait_ge(s_wp, 16 * 3)
                V.tensor_scalar(w_out_sb[:, :, :], w_out_sb[:, :, :], 0.5, None, ALU.mult).then_inc(s_prep, 1)

            seq = {}

            def sequence(b):
                if not is0(b):
                    dve.wait_ge(s_st, NU * MC * b)
                V.memset(hst[:, :, :], 0.0).then_inc(s_rst, 1)
                seq["now"] = b

            def finish(i, par, n):
                for b, s in due(AT["in"], n, i, SILU):
                    silu(i + s, (par + s) % 2, b)
                for b, s in due(AT["gate"], n, i, GATE):
                    gate(i + s, (par + s) % 2, b)
                for pair, s in due(LOG_AT, n, i, ADD):
                    add_log(i + s, pair)
                for b, s in due(YG_AT, n, i):
                    gated(i + s, (par + s) % 2, b)
                for _, s in due(EVAC_AT, n, i):
                    residual(i + s)

            def body(i, par):
                for n in range(NU):
                    steps = [[] for _ in range(KC)]
                    for b, s in due(AT["in"], n, i, TAP):
                        for step in range(1, KC):
                            steps[step].append(lambda b=b, s=s, step=step: conv(i + s, (par + s) % 2, b, step))
                    if n == 0:
                        if not is0(i):
                            dve.wait_ge(s_st, NU * i)
                        dve.wait_ge(s_rst, seq["now"] + 1)
                    dve.wait_ge(s_m1, NU * i + n + 1)
                    if not (is0(i) and n < NH):
                        dve.wait_ge(s_r, NU * i + n - NH + 1)
                    scans(i, n, 0)
                    for step in steps[1]:
                        step()
                    scans(i, n, 1)
                    for step in steps[2]:
                        step()
                    if n > 0:
                        times_c(i, n - 1)
                    elif not is0(i):
                        times_c(i - 1, NU - 1)
                    for step in steps[3]:
                        step()
                    finish(i, par, n)

            def epilogue():
                times_c(LAST, NU - 1)
                for b, at in enumerate(YG_AT):
                    if at >= NU:
                        gated(LAST, LAST % 2, b)
                residual(LAST)

            over_chunks(dve, prologue, body, sequence, epilogue)

        @block.tensor
        def _(pe):
            M = nc.tensor

            def evacuated(kind, b, c):
                if kind == "in":
                    pe.wait_ge(s_cq, ND * c + b + 1)
                elif kind == "bc":
                    pe.wait_ge(s_bc, 16 * (c + 1))
                elif kind == "dt":
                    pe.wait_ge(s_rl, ND * c + b + 1)
                else:
                    pe.wait_ge(s_zs, ND * c + b + 1)

            def bank_free(kind, b, c):
                s = shift(kind, b)
                if is0(c) and s:
                    at = first_order.index((kind, b)) - NP
                    if at >= 0:
                        evacuated(*first_order[at], 0)
                    else:
                        pe.wait_ge(s_cen, 2 * DI // 512)
                    return
                i, at = c - s, order.index((kind, b, s)) - NP
                if at < 0 and is0(i):
                    evacuated(*first_order[at], 0)
                    return
                if order[at][0] == "skip":
                    at -= NP
                evacuated(order[at][0], order[at][1], i + order[at][2] - (1 if at < 0 else 0))

            def input_product(c, cp, b):
                bank_free("in", b, c)
                if b == 0:
                    pe.wait_ge(s_ht[cp], 8 * (c - cp) + 16)
                ps = bank("in", b, c, cp)
                for f in range(NB):
                    ins = M.matmul(ps[:, 0:TH], w_in_sb[:, f, b * P:(b + 1) * P], hT[:, cp, f, :],
                                   start=(f == 0), stop=(f == NB - 1))
                ins.then_inc(s_pi, 1)

            def gate_product(c, cp, b):
                bank_free("gate", b, c)
                ps = bank("gate", b, c, cp)
                for f in range(NB):
                    ins = M.matmul(ps[:, 0:T], w_in_sb[:, f, DI + b * P:DI + (b + 1) * P], hT[:, cp, f, PAD_L:PAD_L + T],
                                   start=(f == 0), stop=(f == NB - 1))
                ins.then_inc(s_pz, 1)

            def bc_product(c, cp):
                bank_free("bc", 0, c)
                pe.wait_ge(s_u, ND * (c + 1))
                for k in range(ND):
                    ins = M.matmul(bank("bc", 0, c, cp)[0:2 * DS, 0:T], w_x_sb[:, k, :], u[:, cp, k, :],
                                   start=(k == 0), stop=(k == ND - 1))
                ins.then_inc(s_pb, 1)

            def dt_products(c, cp, b, ks):
                if ks[0] == 0:
                    bank_free("dt", b, c)
                    pe.wait_ge(s_u, ND * (c + 1))
                for k in ks:
                    ins = M.matmul(bank("dt", b, c, cp)[:, 0:T], w_dt_sb[:, k, b * P:(b + 1) * P],
                                   u[:, cp, k, :], start=(k == 0), stop=(k == ND - 1), skip_group_check=True)
                if ks[-1] == ND - 1:
                    ins.then_inc(s_pd, 1)

            def out_product(c, b):
                pe.wait_ge(s_g, ND * c + b + 1)
                if b == 0 and not is0(c):
                    pe.wait_ge(s_o, c)
                for j in range(TJ):
                    ins = M.matmul(ps_o[j][:, :], gy[:, b % 2, j * P:(j + 1) * P], w_out_sb[:, b, :],
                                   start=(b == 0), stop=(b == ND - 1), skip_group_check=True)
                ins.then_inc(s_po, 1)

            def sum_states(c, n):
                b, g = divmod(n, NG)
                if g == 0 and (b >= 2 or not is0(c)):
                    pe.wait_ge(s_yd, ND * c + b - 1)
                if PAIRED[n]:
                    pe.wait_ge(s_pr, sum(PAIRED) * c + sum(PAIRED[:n + 1]))
                else:
                    pe.wait_ge(s_m2, NU * c + n + 1)
                states = SG // 2 if PAIRED[n] else SG
                for k in range(states):
                    ins = M.matmul(ps_y[b % 2][:, 0:T], ident[:, :], hp[:, n % NH, k, :],
                                   start=(g == 0 and k == 0), stop=(g == NG - 1 and k == states - 1),
                                   skip_group_check=True)
                ins.then_inc(s_r, 1)

            def prologue():
                pe.wait_ge(s_id, 3)
                for c in range(2 * DI // 512):
                    pe.wait_ge(s_w[512 * c // DI], 16)
                    if c >= 2:
                        pe.wait_ge(s_cen, c - 1)
                    for f in range(NB):
                        ins = M.matmul(ps_m[c % 2][:, :], mean_w, w_in_sb[:, f, 512 * c:512 * (c + 1)],
                                       start=(f == 0), stop=(f == NB - 1))
                    ins.then_inc(s_mean, 1)
                for kind, b in first_order:
                    if kind == "in":
                        input_product(0, 0, b)
                    elif kind == "bc":
                        pe.wait_ge(s_wp, 16 * 3)
                        bc_product(0, 0)
                    else:
                        dt_products(0, 0, b, range(ND))
                pe.wait_ge(s_prep, 3)

            def body(i, par):
                for n in range(NU):
                    for b, s in due(OUT_AT, n, i):
                        out_product(i + s, b)
                    for b, s in due(AT["dt"], n, i):
                        if not (is0(i + s) and shift("dt", b)):
                            dt_products(i + s, (par + s) % 2, b, range(DT_EARLY, ND))
                    for b, s in due(AT["bc"], n, i):
                        bc_product(i + s, (par + s) % 2)
                    for b, s in due(AT["gate"], n, i):
                        gate_product(i + s, (par + s) % 2, b)
                    for b, s in due(AT["in"], n, i):
                        input_product(i + s, (par + s) % 2, b)
                    for b, s in due(AT["dt0"], n, i):
                        dt_products(i + s, (par + s) % 2, b, range(DT_EARLY))
                    if n >= SUM_LAG:
                        sum_states(i, n - SUM_LAG)
                    elif not is0(i):
                        sum_states(i - 1, NU + n - SUM_LAG)

            def epilogue():
                for n in range(NU, NU + NG + SUM_LAG + 2):
                    for b, at in enumerate(OUT_AT):
                        if at == n:
                            out_product(LAST, b)
                    if n - SUM_LAG < NU:
                        sum_states(LAST, n - SUM_LAG)

            over_chunks(pe, prologue, body, None, epilogue)


def program(nc, inp, w_in, conv_w, conv_b, w_x, w_dt, b_dt, w_out, a_mat, d_vec, w_r, w_k, w_v, mu_r, mu_k, out):
    xs = nc.dram_tensor("xs_scratch", (BATCH, SEQ, DM), F32).ap()
    x2 = nc.dram_tensor("x2_scratch", (BATCH, SEQ, DM), F32).ap()
    hT_pad = nc.dram_tensor("hT_scratch", (P, NB, BATCH * ROW + TAIL), F32).ap()
    bc_dram = nc.dram_tensor("bc_scratch", (2 * DS, T), F32).ap()
    ffn_phase(nc, "f1", inp, w_r, w_k, w_v, mu_r, mu_k, xs, hT_pad)
    mixer_phase(nc, hT_pad, xs, w_in, conv_w, conv_b, w_x, w_dt, b_dt, w_out, a_mat, d_vec, bc_dram, x2)
    ffn_phase(nc, "f2", x2, w_r, w_k, w_v, mu_r, mu_k, out)


_INS = ["L0_attn_inp", "L0_attn_W_in", "L0_attn_conv_w", "L0_attn_conv_b", "L0_attn_W_x", "L0_attn_W_dt",
        "L0_attn_b_dt", "L0_attn_W_out", "L0_attn_A", "L0_attn_D", "L0_ffn_W_r", "L0_ffn_W_k", "L0_ffn_W_v",
        "L0_ffn_mu_r", "L0_ffn_mu_k"]


def kernel(**inputs):
    import numpy as np
    import concourse.bacc as bacc
    from concourse.bass_utils import run_bass_kernel_spmd

    nc = bacc.Bacc("TRN2", target_bir_lowering=False, num_devices=1)
    arrays, args = {}, []
    for name in _INS:
        a = np.ascontiguousarray(inputs[name])
        arrays[f"in_{name}"] = a
        args.append(nc.dram_tensor(f"in_{name}", a.shape, mybir.dt.from_np(a.dtype), kind="ExternalInput").ap())
    args.append(nc.dram_tensor("out_dram", (BATCH, SEQ, DM), F32, kind="ExternalOutput").ap())
    program(nc, *args)
    r = run_bass_kernel_spmd(nc, [arrays], core_ids=[0])
    return r.results[0]["out_dram"]
```
